# Optimizing a Trainium2 kernel written in Bass

```python
import numpy as np
import jax
import jax.numpy as jnp

def _softmax(x, axis=-1):
    return jax.nn.softmax(x, axis=axis)

def _gelu(x):
    return jax.nn.gelu(x, approximate=True)

def _silu(x):
    return jax.nn.silu(x)

def _sigmoid(x):
    return jax.nn.sigmoid(x)

def _layernorm(x, axis=-1, eps=1e-05):
    m = jnp.mean(x, axis=axis, keepdims=True)
    v = jnp.var(x, axis=axis, keepdims=True)
    return (x - m) / jnp.sqrt(v + eps)

def _scatter_add(tgt, idx, src, axis=0):
    return tgt.at[idx].add(src)

def _segment_sum(src, seg, n):
    return jax.ops.segment_sum(src, seg, n)
kernel_name = 'mk_seq_preln_d1_jaxref_r2_62d0aa'

def setup_inputs(seed: int=0):
    np.random.seed(seed)
    _w = jnp.asarray

    def _L0_attn_setup():
        import jax, jax.numpy as jnp
        import numpy as np
        C = 1024
        A = 1024
        HS = 64
        H = A // HS
        DMIX = 32
        DDEC = 64
        B, T = (2, 1024)
        EPS = 1e-05 * 8.0 ** 2
        key = jax.random.key(seed)
        ks = jax.random.split(key, 20)
        n = lambda i, shape, s=0.02: jax.random.normal(ks[i], shape, dtype=jnp.float32) * s
        return dict(hidden=jax.random.normal(ks[0], (B, T, C), dtype=jnp.float32), time_maa_x=n(1, (1, 1, C), 0.5), time_maa_w=n(2, (1, 1, C), 0.5), time_maa_k=n(3, (1, 1, C), 0.5), time_maa_v=n(4, (1, 1, C), 0.5), time_maa_r=n(5, (1, 1, C), 0.5), time_maa_g=n(6, (1, 1, C), 0.5), time_maa_w1=n(7, (C, DMIX * 5)), time_maa_w2=n(8, (5, DMIX, C)), time_decay=n(9, (1, 1, A), 0.5), time_decay_w1=n(10, (C, DDEC)), time_decay_w2=n(11, (DDEC, A)), time_faaaa=n(12, (H, HS), 0.5), W_r=n(13, (A, C)), W_k=n(14, (A, C)), W_v=n(15, (A, C)), W_g=n(16, (A, C)), W_o=n(17, (C, A)), ln_gamma=jnp.ones((C,), jnp.float32), ln_beta=jnp.zeros((C,), jnp.float32))
    _L0_attn_in = _L0_attn_setup()

    def _L0_ffn_setup():
        import math
        import jax, jax.numpy as jnp
        import numpy as np
        DIM = 1024
        RANK = 8
        B, T = (4, 2048)

        def _orthogonal(key, n):
            a = jax.random.normal(key, (n, n), dtype=jnp.float32)
            q, r = jnp.linalg.qr(a)
            q = q * jnp.sign(jnp.diagonal(r))[None, :]
            return q
        key = jax.random.key(seed)
        kx, kf = jax.random.split(key)
        x = jax.random.normal(kx, (B, T, DIM), dtype=jnp.float32)
        fkeys = jax.random.split(kf, RANK)
        factors = jnp.stack([_orthogonal(fkeys[r], DIM) * (r + 1) ** (-0.5) for r in range(RANK)])
        bias = jnp.zeros((DIM,), dtype=jnp.float32)
        return {'x': x, 'factors': factors, 'bias': bias}
    _L0_ffn_in = _L0_ffn_setup()
    _d = {'L0_attn_hidden': _L0_attn_in['hidden'], 'L0_attn_time_maa_x': _L0_attn_in['time_maa_x'], 'L0_attn_time_maa_w': _L0_attn_in['time_maa_w'], 'L0_attn_time_maa_k': _L0_attn_in['time_maa_k'], 'L0_attn_time_maa_v': _L0_attn_in['time_maa_v'], 'L0_attn_time_maa_r': _L0_attn_in['time_maa_r'], 'L0_attn_time_maa_g': _L0_attn_in['time_maa_g'], 'L0_attn_time_maa_w1': _L0_attn_in['time_maa_w1'], 'L0_attn_time_maa_w2': _L0_attn_in['time_maa_w2'], 'L0_attn_time_decay': _L0_attn_in['time_decay'], 'L0_attn_time_decay_w1': _L0_attn_in['time_decay_w1'], 'L0_attn_time_decay_w2': _L0_attn_in['time_decay_w2'], 'L0_attn_time_faaaa': _L0_attn_in['time_faaaa'], 'L0_attn_W_r': _L0_attn_in['W_r'], 'L0_attn_W_k': _L0_attn_in['W_k'], 'L0_attn_W_v': _L0_attn_in['W_v'], 'L0_attn_W_g': _L0_attn_in['W_g'], 'L0_attn_W_o': _L0_attn_in['W_o'], 'L0_attn_ln_gamma': _L0_attn_in['ln_gamma'], 'L0_attn_ln_beta': _L0_attn_in['ln_beta'], 'L0_ffn_factors': _L0_ffn_in['factors'], 'L0_ffn_bias': _L0_ffn_in['bias']}
    _x0 = _d['L0_attn_hidden']
    _d['L0_attn_hidden'] = jax.random.normal(jax.random.fold_in(jax.random.key(seed), 1), (1, 4096, 1024), dtype=_x0.dtype)
    del _x0
    return _d

def reference(L0_attn_hidden, L0_attn_time_maa_x, L0_attn_time_maa_w, L0_attn_time_maa_k, L0_attn_time_maa_v, L0_attn_time_maa_r, L0_attn_time_maa_g, L0_attn_time_maa_w1, L0_attn_time_maa_w2, L0_attn_time_decay, L0_attn_time_decay_w1, L0_attn_time_decay_w2, L0_attn_time_faaaa, L0_attn_W_r, L0_attn_W_k, L0_attn_W_v, L0_attn_W_g, L0_attn_W_o, L0_attn_ln_gamma, L0_attn_ln_beta, L0_ffn_factors, L0_ffn_bias):

    def _L0_attn_ref(hidden, time_maa_x, time_maa_w, time_maa_k, time_maa_v, time_maa_r, time_maa_g, time_maa_w1, time_maa_w2, time_decay, time_decay_w1, time_decay_w2, time_faaaa, W_r, W_k, W_v, W_g, W_o, ln_gamma, ln_beta):
        import jax, jax.numpy as jnp
        import numpy as np
        C = 1024
        A = 1024
        HS = 64
        H = A // HS
        DMIX = 32
        DDEC = 64
        B, T = (2, 1024)
        EPS = 1e-05 * 8.0 ** 2
        Bq, Tq, Cq = hidden.shape
        shifted = jnp.pad(hidden, ((0, 0), (1, 0), (0, 0)))[:, :-1]
        xx = shifted - hidden
        xxx = hidden + xx * time_maa_x
        z = jnp.tanh(jnp.einsum('btc,cd->btd', xxx, time_maa_w1)).reshape(Bq, Tq, 5, DMIX)
        mix = jnp.einsum('btfd,fdc->fbtc', z, time_maa_w2)
        mw, mk, mv, mr, mg = (mix[0], mix[1], mix[2], mix[3], mix[4])
        xw = hidden + xx * (time_maa_w + mw)
        xk = hidden + xx * (time_maa_k + mk)
        xv = hidden + xx * (time_maa_v + mv)
        xr = hidden + xx * (time_maa_r + mr)
        xg = hidden + xx * (time_maa_g + mg)
        r = jnp.einsum('btc,ac->bta', xr, W_r)
        k = jnp.einsum('btc,ac->bta', xk, W_k)
        v = jnp.einsum('btc,ac->bta', xv, W_v)
        g = jax.nn.silu(jnp.einsum('btc,ac->bta', xg, W_g))
        dd = jnp.einsum('btd,da->bta', jnp.tanh(jnp.einsum('btc,cd->btd', xw, time_decay_w1)), time_decay_w2) + time_decay
        w = jnp.exp(-jnp.exp(dd))
        rh = r.reshape(Bq, Tq, H, HS).transpose(1, 0, 2, 3)
        kh = k.reshape(Bq, Tq, H, HS).transpose(1, 0, 2, 3)
        vh = v.reshape(Bq, Tq, H, HS).transpose(1, 0, 2, 3)
        wh = w.reshape(Bq, Tq, H, HS).transpose(1, 0, 2, 3)
        u = time_faaaa

        def step(S, inputs):
            r_t, k_t, v_t, w_t = inputs
            kv = k_t[..., :, None] * v_t[..., None, :]
            out_t = jnp.einsum('bhn,bhnm->bhm', r_t, u[None, :, :, None] * kv + S)
            S = kv + w_t[..., :, None] * S
            return (S, out_t)
        S0 = jnp.zeros((Bq, H, HS, HS), dtype=hidden.dtype)
        _, outs = jax.lax.scan(step, S0, (rh, kh, vh, wh))
        out = outs.transpose(1, 0, 2, 3)
        mean = out.mean(-1, keepdims=True)
        var = out.var(-1, keepdims=True)
        out = (out - mean) * jax.lax.rsqrt(var + EPS)
        out = out.reshape(Bq, Tq, Cq) * ln_gamma + ln_beta
        out = out * g
        return jnp.einsum('bta,ca->btc', out, W_o)

    def _L0_ffn_ref(x, factors, bias):
        import math
        import jax, jax.numpy as jnp
        import numpy as np
        DIM = 1024
        RANK = 8
        B, T = (4, 2048)

        def _orthogonal(key, n):
            a = jax.random.normal(key, (n, n), dtype=jnp.float32)
            q, r = jnp.linalg.qr(a)
            q = q * jnp.sign(jnp.diagonal(r))[None, :]
            return q
        rank = factors.shape[0]
        mixed = jnp.einsum('btd,rde->bte', x, factors)
        mixed = mixed / math.sqrt(rank) + bias
        return mixed
    x = L0_attn_hidden
    x = x + _L0_attn_ref(_layernorm(x, axis=-1), L0_attn_time_maa_x, L0_attn_time_maa_w, L0_attn_time_maa_k, L0_attn_time_maa_v, L0_attn_time_maa_r, L0_attn_time_maa_g, L0_attn_time_maa_w1, L0_attn_time_maa_w2, L0_attn_time_decay, L0_attn_time_decay_w1, L0_attn_time_decay_w2, L0_attn_time_faaaa, L0_attn_W_r, L0_attn_W_k, L0_attn_W_v, L0_attn_W_g, L0_attn_W_o, L0_attn_ln_gamma, L0_attn_ln_beta)
    x = x + _L0_ffn_ref(_layernorm(x, axis=-1), L0_ffn_factors, L0_ffn_bias)
    return x

_drawn_inputs = setup_inputs


def setup_inputs(seed=0):
    import zlib

    import numpy as np

    out = dict(_drawn_inputs(seed))
    spreads = {'L0_attn_ln_gamma': (1.0, 0.2), 'L0_attn_ln_beta': (0.0, 0.29), 'L0_ffn_bias': (0.0, 0.1)}
    factors = {'L0_attn_time_maa_w': 8.0, 'L0_attn_time_decay_w1': 4.577, 'L0_attn_time_decay_w2': 4.569}
    for name, (base, spread) in spreads.items():
        noise = np.random.default_rng([zlib.crc32(name.encode()), seed]).standard_normal(out[name].shape)
        drawn = base * np.exp(spread * noise) if base else spread * noise
        out[name] = jnp.asarray(drawn.astype(out[name].dtype))
    for name, factor in factors.items():
        out[name] = (out[name] * factor).astype(out[name].dtype)
    return out
```

```python
from contextlib import ExitStack

import concourse.bass as bass
from concourse import mybir

F32 = mybir.dt.float32
F32R = mybir.dt.float32r
I32 = mybir.dt.int32
ALU = mybir.AluOpType
ACT = mybir.ActivationFunctionType
AX_X = mybir.AxisListType.X

P = 128
C = 1024
T = 4096
HEAD = 64
H = C // HEAD
CB = C // P
DMIX = 32
NMIX = 5
DDEC = 64
RANK = 8
WIN = 512
NW = T // WIN
SUB = WIN // P
LN_EPS = 1e-5
GN_EPS = 1e-5 * 8.0 ** 2
CHUNK = 128
NCH = T // CHUNK
LEVELS = 7


class Phase:

    def __init__(self, nc, prefix):
        self.nc, self.prefix, self.held = nc, prefix, []

    def __enter__(self):
        return self

    def semaphore(self, name):
        self.held.append(self.nc.alloc_semaphore(self.prefix + name))
        return self.held[-1]

    def counter(self, name, per=1):
        return Counter(self.semaphore(name), per)

    def __exit__(self, *error):
        if error[0] is None:
            self.nc.clear_and_free_semaphores(self.held)
            self.nc.all_engine_barrier()


class Counter:

    def __init__(self, sem, per=1):
        self.sem, self.per = sem, per

    def grant(self, eng):
        eng.sem_inc(self.sem, self.per)

    def now(self, step, k=None):
        return self.per * (step + 1) + (self.per if k is None else k + 1)

    def prev(self, step, k=None):
        return self.per * step + (self.per if k is None else k + 1)


def columns(vector_dram):
    return vector_dram.rearrange("(b p) -> p b", p=P)


def hop(eng, passed):
    eng.sem_inc(passed, 1)


def norm_phase(nc, x, maa_x, w1, ident_dram, factors, hT, zs, factors_sum):
    with ExitStack() as ctx:
        sb = lambda name, shape, dt=F32: ctx.enter_context(nc.sbuf_tensor(name, shape, dt))
        phase = ctx.enter_context(Phase(nc, "n_"))
        sig, sem = phase.counter, phase.semaphore
        ident = sb("n_ident", [P, P])
        maa = sb("n_maa", [P, CB])
        w1s = sb("n_w1", [P, CB, NMIX * DMIX])
        xb = sb("n_x", [P, SUB, C])
        stats = sb("n_stats", [P, SUB, 12])
        mv = sb("n_mv", [P, SUB, 2])
        sd = sb("n_sd", [P, SUB])
        rstd = sb("n_rstd", [P, SUB])
        nmr = sb("n_nmr", [P, SUB])
        eps = sb("n_eps", [P, 1])
        xn = sb("n_xn", [P, SUB, C])
        h = sb("n_h", [P, CB, WIN + 1])
        zero = sb("n_zero", [P, CB])
        xx = sb("n_xx", [P, 2, WIN])
        xxx = sb("n_xxx", [P, 4, WIN])
        za, zb = sb("n_za", [P, WIN]), sb("n_zb", [DMIX, WIN])
        za_hi, zb_hi = sb("n_zahi", [P, WIN], F32R), sb("n_zbhi", [DMIX, WIN], F32R)
        za_lo, zb_lo = sb("n_zalo", [P, WIN], F32R), sb("n_zblo", [DMIX, WIN], F32R)
        fac = sb("n_fac", [P, 4, C])
        fsum = sb("n_fsum", [P, C])
        ps_t = [ctx.enter_context(nc.psum_tensor(f"n_pst{b}", [P, WIN], F32)) for b in range(4)]
        ps_za = ctx.enter_context(nc.psum_tensor("n_psza", [P, WIN], F32))
        ps_zb = ctx.enter_context(nc.psum_tensor("n_pszb", [DMIX, WIN], F32))

        consts, zero_stored, zeroed = sem("consts"), sem("zero_stored"), sem("zeroed")
        x_loaded = [sem(f"x_loaded{j}") for j in range(SUB)]
        h_stored = [sig(f"h_stored{b}", 16) for b in range(CB)]
        z_stored = sig("z_stored", 16 * 6)
        passed, pool_passed = sem("passed"), sem("pool_passed")
        fac_loaded = [sem(f"fac_loaded{n}") for n in range(4)]
        sum_stored = sig("sum_stored", 16)
        added = sig("added", RANK - 1)
        stat = sig("stat", 2 * SUB)
        aggr = sig("aggr", SUB)
        rooted = sig("rooted")
        scaled = sig("scaled", 2)
        xn_ready = sig("xn_ready", SUB)
        turned = sig("turned", CB)
        h_ready = sig("h_ready", CB)
        xx_ready = sig("xx_ready", CB)
        carried = sig("carried", CB)
        xxx_ready = sig("xxx_ready", CB)
        z_step = sig("z_step", CB)
        z_tanh = sig("z_tanh", 2)
        z_hi = sig("z_hi", 2)
        z_lo = sig("z_lo", 2)
        block = ctx.enter_context(nc.Block())

        @block.sync
        def _(sp):
            sum_stored.grant(sp)
            sp.dma_start(ident[:], ident_dram).then_inc(consts, 16)
            with nc.allow_non_contiguous_dma(reason="one vector of channels"):
                sp.dma_start(maa[:], columns(maa_x)).then_inc(consts, 16)
            sp.dma_start(w1s[:], w1.rearrange("(b p) d -> p b d", p=P)).then_inc(consts, 16)
            sp.wait_ge(zeroed, 3)
            with nc.allow_non_contiguous_dma(reason="the zero token in front"):
                sp.dma_start(hT[:, :, 0], zero[:]).then_inc(zero_stored, 16)

            def load_x(w):
                for j in range(SUB):
                    sp.wait_ge(xn_ready.sem, xn_ready.prev(w, j))
                    sp.dma_start(xb[:, j, :], x[bass.ds(w * WIN + j * P, P), :]).then_inc(x_loaded[j], 16)

            def body(w, last):
                for r in range(RANK):
                    if r < 4:
                        sp.wait_ge(added.sem, added.prev(w, r + 3))
                    else:
                        sp.wait_ge(added.sem, added.now(w, max(r - 5, 0)))
                    sp.dma_start(fac[:, r % 4, :], factors[r, bass.ds(w * P, P), :]).then_inc(fac_loaded[r % 4], 16)
                    if r == 1 and not last:
                        load_x(w + 1)
                sp.wait_ge(added.sem, added.now(w))
                sp.dma_start(factors_sum[bass.ds(w * P, P), :], fsum[:]).then_inc(sum_stored.sem, 16)

            load_x(0)
            with sp.Fori(0, NW - 1) as w:
                body(w, False)
            body(NW - 1, True)
            sp.wait_ge(sum_stored.sem, sum_stored.now(NW - 1))

        @block.gpsimd
        def _(pool):
            for s in (xx_ready, carried, added):
                s.grant(pool)

            def add_factor(w, r):
                pool.wait_ge(fac_loaded[r % 4], 16 * (2 * w + r // 4 + 1))
                if r == 0:
                    return
                if r == 1:
                    pool.wait_ge(sum_stored.sem, sum_stored.prev(w))
                    pool.tensor_tensor(fsum[:], fac[:, 0, :], fac[:, 1, :], ALU.add).then_inc(added.sem, 1)
                else:
                    pool.wait_ge(added.sem, added.now(w, r - 2))
                    pool.tensor_tensor(fsum[:], fsum[:], fac[:, r % 4, :], ALU.add).then_inc(added.sem, 1)

            with pool.Fori(0, NW) as w:
                for b in range(CB):
                    pool.wait_ge(h_ready.sem, h_ready.now(w, b))
                    if b >= 2:
                        pool.wait_ge(xxx_ready.sem, xxx_ready.now(w, b - 2))
                    else:
                        pool.wait_ge(xxx_ready.sem, xxx_ready.prev(w, CB - 2 + b))
                    pool.wait_ge(carried.sem, carried.prev(w, b))
                    pool.tensor_tensor(xx[:, b % 2, :], h[:, b, 0:WIN], h[:, b, 1:WIN + 1],
                                       ALU.subtract).then_inc(xx_ready.sem, 1)
                    pool.wait_ge(xx_ready.sem, xx_ready.now(w, b))
                    hop(pool, pool_passed)
                    pool.tensor_copy(h[:, b, 0:1], h[:, b, WIN:WIN + 1]).then_inc(carried.sem, 1)
                    add_factor(w, b)

        @block.vector
        def _(dve):
            dve.memset(h[:], 0.0).then_inc(zeroed, 1)
            dve.memset(zero[:], 0.0).then_inc(zeroed, 1)
            dve.memset(eps[:], LN_EPS).then_inc(zeroed, 1)
            for s in (stat, aggr, scaled, xxx_ready, z_lo):
                s.grant(dve)
            dve.wait_ge(consts, 48)
            with dve.Fori(0, NW) as w:
                for j in range(SUB):
                    dve.wait_ge(x_loaded[j], 16 * (w + 1))
                    if j == 0:
                        dve.wait_ge(aggr.sem, aggr.prev(w))
                    for half in range(2):
                        dve.bn_stats(stats[:, j, 6 * half:6 * half + 6],
                                     xb[:, j, 512 * half:512 * half + 512]).then_inc(stat.sem, 1)
                dve.wait_ge(scaled.sem, scaled.prev(w))
                for j in range(SUB):
                    dve.wait_ge(stat.sem, stat.now(w, 2 * j + 1))
                    hop(dve, passed)
                    dve.bn_aggr(mv[:, j, :], stats[:, j, :]).then_inc(aggr.sem, 1)
                dve.wait_ge(rooted.sem, rooted.now(w))
                dve.wait_ge(xn_ready.sem, xn_ready.prev(w))
                dve.reciprocal(rstd[:], sd[:]).then_inc(scaled.sem, 1)
                dve.wait_ge(scaled.sem, scaled.now(w, 0))
                dve.scalar_tensor_tensor(nmr[:], mv[:, :, 0], -1.0, rstd[:], ALU.mult,
                                         ALU.mult).then_inc(scaled.sem, 1)
                for b in range(CB):
                    dve.wait_ge(xx_ready.sem, xx_ready.now(w, b))
                    if b >= 4:
                        dve.wait_ge(z_step.sem, z_step.now(w, b - 4))
                    else:
                        dve.wait_ge(z_step.sem, z_step.prev(w, CB - 4 + b))
                    dve.scalar_tensor_tensor(xxx[:, b % 4, :], xx[:, b % 2, :], maa[:, b:b + 1],
                                             h[:, b, 1:WIN + 1], ALU.mult,
                                             ALU.add).then_inc(xxx_ready.sem, 1)
                for n, (lo, full, hi) in enumerate(((za_lo, za, za_hi), (zb_lo, zb, zb_hi))):
                    dve.wait_ge(z_hi.sem, z_hi.now(w, n))
                    dve.wait_ge(z_stored.sem, z_stored.prev(w))
                    dve.tensor_tensor(lo[:], full[:], hi[:].bitcast(F32),
                                      ALU.subtract).then_inc(z_lo.sem, 1)

        @block.scalar
        def _(act):
            for s in (rooted, xn_ready, h_ready, z_tanh, z_hi, z_stored, *h_stored):
                s.grant(act)
            act.wait_ge(zeroed, 3)
            with act.Fori(0, NW) as w:
                act.wait_ge(aggr.sem, aggr.now(w))
                act.activation(sd[:], mv[:, :, 1], ACT.Sqrt, bias=eps[:]).then_inc(rooted.sem, 1)
                act.wait_ge(scaled.sem, scaled.now(w))
                act.wait_ge(turned.sem, turned.prev(w))
                for j in range(SUB):
                    act.activation(xn[:, j, :], xb[:, j, :], ACT.Identity, bias=nmr[:, j:j + 1],
                                   scale=rstd[:, j:j + 1]).then_inc(xn_ready.sem, 1)
                for b in range(CB):
                    act.wait_ge(turned.sem, turned.now(w, b))
                    act.wait_ge(carried.sem, carried.prev(w, b))
                    act.wait_ge(xxx_ready.sem, xxx_ready.prev(w, b))
                    act.wait_ge(h_stored[b].sem, h_stored[b].prev(w))
                    act.copy(h[:, b, 1:WIN + 1], ps_t[b % 4][:]).then_inc(h_ready.sem, 1)
                    act.wait_ge(h_ready.sem, h_ready.now(w, b))
                    act.dma_start(hT[:, b, bass.ds(w * WIN + 1, WIN)],
                                  h[:, b, 1:WIN + 1]).then_inc(h_stored[b].sem, 16)
                act.wait_ge(z_step.sem, z_step.now(w))
                act.wait_ge(z_lo.sem, z_lo.prev(w))
                act.activation(za[:], ps_za[:], ACT.Tanh).then_inc(z_tanh.sem, 1)
                act.activation(zb[:], ps_zb[:], ACT.Tanh).then_inc(z_tanh.sem, 1)
                act.wait_ge(z_stored.sem, z_stored.prev(w))
                for n, (hi, full) in enumerate(((za_hi, za), (zb_hi, zb))):
                    act.wait_ge(z_tanh.sem, z_tanh.now(w, n))
                    act.copy(hi[:], full[:]).then_inc(z_hi.sem, 1)
                act.wait_ge(z_lo.sem, z_lo.now(w))
                act.wait_ge(z_hi.sem, z_hi.now(w))
                cols = bass.ds(w * WIN, WIN)
                for part, (a, bb) in enumerate(((za_hi, zb_hi), (za_lo, zb_lo), (za_hi, zb_hi))):
                    rows = slice(part * DMIX, part * DMIX + DMIX)
                    act.dma_start(zs[0:4, rows, cols], a[:].bitcast(F32)).then_inc(z_stored.sem, 16)
                    act.dma_start(zs[4, rows, cols], bb[:].bitcast(F32)).then_inc(z_stored.sem, 16)
            act.wait_ge(z_stored.sem, z_stored.now(NW - 1))
            act.wait_ge(zero_stored, 16)
            for s in h_stored:
                act.wait_ge(s.sem, s.now(NW - 1))

        @block.tensor
        def _(pe):
            for s in (turned, z_step):
                s.grant(pe)
            pe.wait_ge(consts, 48)
            with pe.Fori(0, NW) as w:
                pe.wait_ge(xn_ready.sem, xn_ready.now(w))
                for b in range(CB):
                    if b >= 4:
                        pe.wait_ge(h_ready.sem, h_ready.now(w, b - 4))
                    else:
                        pe.wait_ge(h_ready.sem, h_ready.prev(w, CB - 4 + b))
                    for j in range(SUB):
                        mm = pe.transpose(ps_t[b % 4][:, j * P:(j + 1) * P],
                                          xn[:, j, b * P:(b + 1) * P], ident[:])
                    mm.then_inc(turned.sem, 1)
                pe.wait_ge(z_tanh.sem, z_tanh.prev(w))
                for b in range(CB):
                    pe.wait_ge(xxx_ready.sem, xxx_ready.now(w, b))
                    pe.matmul(ps_za[:], w1s[:, b, 0:P], xxx[:, b % 4, :], start=b == 0, stop=b == CB - 1)
                    pe.matmul(ps_zb[:], w1s[:, b, P:], xxx[:, b % 4, :], start=b == 0,
                              stop=b == CB - 1).then_inc(z_step.sem, 1)


def load_split(nc, ctx, phase, groups):
    pieces = [(dram[:, b, :], hi[:, b, :], lo[:, b, :]) for dram, hi, lo in groups for b in range(dram.shape[1])]
    width = max(src.shape[1] for src, _, _ in pieces)
    rows = max(src.shape[0] for src, _, _ in pieces)
    slot = ctx.enter_context(nc.sbuf_tensor(phase.prefix + "wslot", [rows, 2, width], F32))
    loaded = [phase.semaphore(f"wloaded{n}") for n in range(2)]
    high, low = phase.semaphore("whigh"), phase.semaphore("wlow")

    def part(n):
        src, hi, lo = pieces[n]
        return src, slot[0:src.shape[0], n % 2, 0:src.shape[1]], hi, lo

    def load(sp):
        for n in range(len(pieces)):
            src, full, _, _ = part(n)
            if n >= 2:
                sp.wait_ge(low, n - 1)
            sp.dma_start(full, src).then_inc(loaded[n % 2], 16)

    def take_high(act):
        for n in range(len(pieces)):
            _, full, hi, _ = part(n)
            act.wait_ge(loaded[n % 2], 16 * (n // 2 + 1))
            act.copy(hi, full).then_inc(high, 1)

    def take_low(dve):
        for n in range(len(pieces)):
            _, full, hi, lo = part(n)
            dve.wait_ge(high, n + 1)
            dve.tensor_tensor(lo, full, hi.bitcast(F32), ALU.subtract).then_inc(low, 1)

    return load, take_high, take_low, (low, len(pieces))


def projection_phase(nc, kind, hT, zs_f, maa, w2_f, out, weight=None, decay=None):
    with ExitStack() as ctx:
        pre = f"p{out.tensor.name}_"
        sb = lambda name, shape, dt=F32: ctx.enter_context(nc.sbuf_tensor(pre + name, shape, dt))
        phase = ctx.enter_context(Phase(nc, pre))
        sig, sem = phase.counter, phase.semaphore
        split = kind != "w"
        maas = sb("maa", [P, CB])
        w2 = sb("w2", [3 * DMIX, C], F32R)
        w2_full = sb("w2full", [3 * DMIX, C])
        z = sb("z", [3 * DMIX, T], F32R)
        h = sb("h", [P, CB, WIN + 1])
        xx = sb("xx", [P, 2, WIN])
        prod = sb("prod", [P, 2, WIN])
        stage = sb("stage", [P, 4, WIN])
        if split:
            xf = sb("xf", [P, 2, WIN])
            hi = sb("hi", [P, 2, CB, WIN], F32R)
            lo = sb("lo", [P, 2, CB, WIN], F32R)
            w_hi = sb("whi", [P, CB, C], F32R)
            w_lo = sb("wlo", [P, CB, C], F32R)
            split_load, split_high, split_low, (w_low, n_low) = load_split(
                nc, ctx, phase, [(weight, w_hi, w_lo)])
        else:
            dw1_dram, dw2_dram, bias_dram = decay
            xf = sb("xf", [P, 2 * CB, WIN])
            dw1 = sb("dw1", [P, CB, DDEC])
            dw2 = sb("dw2", [DDEC, C])
            bias = sb("bias", [P, CB])
            td = sb("td", [DDEC, WIN])
            rate = sb("rate", [P, 2, WIN])
        ps_mix = [ctx.enter_context(nc.psum_tensor(pre + f"mix{b}", [P, WIN], F32)) for b in range(2)]
        ps_out = [ctx.enter_context(nc.psum_tensor(pre + f"out{b}", [P, WIN], F32)) for b in range(4)]
        ps_d = ctx.enter_context(nc.psum_tensor(pre + "psd", [DDEC, WIN], F32))

        consts, z_loaded = sem("consts"), sem("z_loaded")
        h_loaded = [sem(f"h_loaded{b}") for b in range(CB)]
        stored = [sig(f"stored{n}", 2 * 16) for n in range(4)]
        w2_ready = sem("w2_ready")
        mixed = sig("mixed", CB)
        xx_ready = sig("xx_ready", CB)
        prod_ready = sig("prod_ready", CB)
        xf_ready = sig("xf_ready", CB)
        hi_ready = sig("hi_ready", CB)
        lo_ready = sig("lo_ready", CB)
        out_done = sig("out_done", CB)
        copied = sig("copied", CB)
        d_done = sig("d_done")
        td_ready = sig("td_ready")
        rated = sig("rated", CB)
        block = ctx.enter_context(nc.Block())
        n_consts = 16 * (5 if split else 8)

        def back(n, k):
            return (k - n) % CB, k < n

        def wait_back(eng, signal, w, k, n):
            j, before = back(n, k)
            eng.wait_ge(signal.sem, signal.prev(w, j) if before else signal.now(w, j))

        def windows(eng, body):
            with eng.Fori(0, NW // 2 - 1) as pair:
                for parity in range(2):
                    body(2 * pair + parity, parity, False)
            body(NW - 2, 0, False)
            body(NW - 1, 1, True)

        @block.sync
        def _(sp):
            for s in stored:
                s.grant(sp)
            with nc.allow_non_contiguous_dma(reason="one vector of channels"):
                sp.dma_start(maas[:], columns(maa)).then_inc(consts, 16)
                if not split:
                    sp.dma_start(bias[:], columns(bias_dram)).then_inc(consts, 16)
            for part in range(3):
                sp.dma_start(w2_full[part * DMIX:(part + 1) * DMIX, :], w2_f).then_inc(consts, 16)
            sp.dma_start(z[:].bitcast(F32), zs_f).then_inc(consts, 16)
            if not split:
                sp.dma_start(dw1[:], dw1_dram.rearrange("(b p) d -> p b d", p=P)).then_inc(consts, 16)
                sp.dma_start(dw2[:], dw2_dram).then_inc(consts, 16)

            def load_h(w, b):
                sp.dma_start(h[:, b, :], hT[:, b, bass.ds(w * WIN, WIN + 1)]).then_inc(h_loaded[b], 16)

            for b in range(CB):
                load_h(0, b)
            if split:
                split_load(sp)
            for b in range(CB):
                sp.wait_ge(xf_ready.sem, xf_ready.now(0, b))
                load_h(1, b)

            def body(w, parity, last):
                for b in range(CB):
                    if not last and not (isinstance(w, int) and w + 2 >= NW):
                        sp.wait_ge(xf_ready.sem, xf_ready.now(w + 1, b))
                        load_h(w + 2, b)
                    sp.wait_ge(copied.sem, copied.now(w, b))
                    if kind == "v":
                        rows = bass.ds(w * WIN + (b // 2) * P, P)
                        dst = out[rows, (b % 2) * WIN:(b % 2 + 1) * WIN]
                    else:
                        dst = out[:, b, bass.ds(w * WIN, WIN)]
                    sp.dma_start(dst, stage[:, b % 4, :]).then_inc(stored[b % 4].sem, 16)

            windows(sp, body)
            for s in stored:
                sp.wait_ge(s.sem, s.now(NW - 1))

        @block.gpsimd
        def _(pool):
            xx_ready.grant(pool)

            def shift(w, b):
                pool.wait_ge(h_loaded[b], 16 * (w + 1))
                wait_back(pool, prod_ready, w, b, 2)
                pool.tensor_tensor(xx[:, b % 2, :], h[:, b, 0:WIN], h[:, b, 1:WIN + 1],
                                   ALU.subtract).then_inc(xx_ready.sem, 1)

            with pool.Fori(0, NW) as w:
                for b in range(CB):
                    shift(w, b)

        @block.vector
        def _(dve):
            for s in (prod_ready, xf_ready, lo_ready):
                s.grant(dve)
            dve.wait_ge(consts, n_consts)
            dve.tensor_copy(w2[:], w2_full[:]).then_inc(w2_ready, 1)
            dve.wait_ge(w2_ready, 1)
            dve.tensor_tensor(w2[2 * DMIX:, :], w2_full[2 * DMIX:, :], w2[2 * DMIX:, :].bitcast(F32),
                              ALU.subtract).then_inc(w2_ready, 1)

            def xf_slot(parity, b):
                return xf[:, b % 2, :] if split else xf[:, parity * CB + b, :]

            def low(w, parity, b):
                dve.wait_ge(hi_ready.sem, hi_ready.now(w, b))
                dve.tensor_tensor(lo[:, parity, b, :], xf_slot(parity, b),
                                  hi[:, parity, b, :].bitcast(F32), ALU.subtract).then_inc(lo_ready.sem, 1)

            def mix(w, parity, b):
                dve.wait_ge(xx_ready.sem, xx_ready.now(w, b))
                dve.wait_ge(mixed.sem, mixed.now(w, b))
                wait_back(dve, xf_ready, w, b, 2)
                dve.scalar_tensor_tensor(prod[:, b % 2, :], ps_mix[b % 2][:], maas[:, b:b + 1],
                                         xx[:, b % 2, :], ALU.add, ALU.mult).then_inc(prod_ready.sem, 1)
                dve.wait_ge(prod_ready.sem, prod_ready.now(w, b))
                if split:
                    wait_back(dve, lo_ready, w, b, 2)
                else:
                    if not isinstance(w, int) or w >= 2:
                        dve.wait_ge(d_done.sem, d_done.prev(w) - 1)
                dve.tensor_tensor(xf_slot(parity, b), prod[:, b % 2, :], h[:, b, 1:WIN + 1],
                                  ALU.add).then_inc(xf_ready.sem, 1)

            def window(w, parity):
                for b in range(CB):
                    mix(w, parity, b)
                    if split and b >= 1:
                        low(w, parity, b - 1)
                if split:
                    low(w, parity, CB - 1)

            window(0, 0)
            if split:
                split_low(dve)

            def body(w, parity, last):
                if not last:
                    if split:
                        dve.wait_ge(out_done.sem, out_done.prev(w))
                    window(w + 1, 1 - parity)

            windows(dve, body)

        @block.scalar
        def _(act):
            for s in (hi_ready, copied, td_ready, rated):
                s.grant(act)

            def high(w, parity, b):
                act.wait_ge(xf_ready.sem, xf_ready.now(w, b))
                act.copy(hi[:, parity, b, :], xf[:, b % 2, :]).then_inc(hi_ready.sem, 1)

            def evacuate(w, b):
                act.wait_ge(out_done.sem, out_done.now(w, b))
                act.wait_ge(stored[b % 4].sem, stored[b % 4].prev(w) if b < 4
                            else stored[b % 4].now(w, 15))
                slot = stage[:, b % 4, :]
                if kind == "w":
                    wait_back(act, copied, w, b, 2)
                    act.activation(rate[:, b % 2, :], ps_out[b % 4][:], ACT.Exp,
                                   bias=bias[:, b:b + 1]).then_inc(rated.sem, 1)
                    act.wait_ge(rated.sem, rated.now(w, b))
                    act.activation(slot, rate[:, b % 2, :], ACT.Exp, scale=-1.0).then_inc(copied.sem, 1)
                elif kind == "g":
                    act.activation(slot, ps_out[b % 4][:], ACT.Silu).then_inc(copied.sem, 1)
                else:
                    act.copy(slot, ps_out[b % 4][:]).then_inc(copied.sem, 1)

            if split:
                for b in range(CB):
                    high(0, 0, b)
                split_high(act)
            else:
                act.wait_ge(consts, n_consts)

            def body(w, parity, last):
                if split:
                    act.wait_ge(out_done.sem, out_done.prev(w))
                else:
                    act.wait_ge(d_done.sem, d_done.now(w))
                    act.wait_ge(out_done.sem, out_done.prev(w))
                    act.activation(td[:], ps_d[:], ACT.Tanh).then_inc(td_ready.sem, 1)
                for b in range(CB):
                    if split and not last:
                        high(w + 1, 1 - parity, b)
                    evacuate(w, b)

            windows(act, body)

        @block.tensor
        def _(pe):
            for s in (mixed, out_done, d_done):
                s.grant(pe)
            pe.wait_ge(consts, n_consts)
            pe.wait_ge(w2_ready, 2)

            def mix(w, b):
                wait_back(pe, prod_ready, w, b, 2)
                pe.matmul(ps_mix[b % 2][:], w2[:, b * P:(b + 1) * P], z[:, bass.ds(w * WIN, WIN)],
                          start=True, stop=True).then_inc(mixed.sem, 1)

            def output(w, parity, n):
                wait_back(pe, copied, w, n, 4)
                if not split:
                    mm = pe.matmul(ps_out[n % 4][:], dw2[:, n * P:(n + 1) * P], td[:], start=True, stop=True)
                    mm.then_inc(out_done.sem, 1)
                    return
                for b in range(CB):
                    if n == 0:
                        pe.wait_ge(lo_ready.sem, lo_ready.now(w, b))
                    for a_hi, b_hi in ((1, 1), (1, 0), (0, 1)):
                        xs, ws = (hi if a_hi else lo), (w_hi if b_hi else w_lo)
                        if kind == "v":
                            left = xs[:, parity, b, (n // 2) * P:(n // 2 + 1) * P]
                            right = ws[:, b, (n % 2) * WIN:(n % 2 + 1) * WIN]
                        else:
                            left, right = ws[:, b, n * P:(n + 1) * P], xs[:, parity, b, :]
                        first, final = b == 0 and a_hi and b_hi, b == CB - 1 and not a_hi
                        mm = pe.matmul(ps_out[n % 4][:], left, right, start=bool(first), stop=bool(final))
                mm.then_inc(out_done.sem, 1)

            for b in range(CB):
                mix(0, b)
            if split:
                pe.wait_ge(w_low, n_low)

            def body(w, parity, last):
                if not split:
                    for b in range(CB):
                        pe.wait_ge(xf_ready.sem, xf_ready.now(w, b))
                        mm = pe.matmul(ps_d[:], dw1[:, b, :], xf[:, parity * CB + b, :],
                                       start=b == 0, stop=b == CB - 1)
                    mm.then_inc(d_done.sem, 1)
                for b in range(CB):
                    if not last:
                        mix(w + 1, b)
                    if not split and b == 0:
                        pe.wait_ge(td_ready.sem, td_ready.now(w))
                    output(w, parity, b)

            windows(pe, body)


def recurrence_phase(nc, rT, kT, wT, gT, v, faaaa, gamma, beta, ident_dram, mask_dram, yT):
    with ExitStack() as ctx:
        sb = lambda name, shape, dt=F32: ctx.enter_context(nc.sbuf_tensor("r_" + name, shape, dt))
        ps = lambda name, shape: ctx.enter_context(nc.psum_tensor("r_" + name, shape, F32))
        phase = ctx.enter_context(Phase(nc, "r_"))
        sig, sem = phase.counter, phase.semaphore
        HALF = CHUNK // 2
        GB = CB // 2

        ident = sb("ident", [P, P])
        masks = sb("masks", [P, LEVELS, HALF], I32)
        bonus = sb("bonus", [P, CB, 2])
        gam, bet = sb("gam", [P, CB]), sb("bet", [P, CB])
        rb, kb, wb, gb = (sb(n, [P, 2, CB, CHUNK]) for n in ("rb", "kb", "wb", "gb"))
        vb = sb("vb", [P, 2, C])
        rbd = sb("rbd", [P, 2, CB, 2 * HALF])
        decays = sb("decays", [P, 2, CB * CHUNK])
        at = sb("at", [P, 2, H, CHUNK])
        rk = sb("rk", [P, CB, CHUNK])
        dsb = sb("dsb", [P, H])
        dv = sb("dv", [P, C])
        kt = sb("kt", [P, C])
        state = sb("state", [P, 2, CB, P])
        ob, cen, sq, nrm = (sb(n, [P, C]) for n in ("ob", "cen", "sq", "nrm"))
        gsum, gmean, gvar, gve, gsd, grs = (sb(n, [P, H]) for n in ("gsum", "gmean", "gvar", "gve", "gsd", "grs"))
        yt, yb = sb("yt", [P, CB, CHUNK]), sb("yb", [P, CB, CHUNK])
        ps_a = [[ps(f"a{s}{g}", [P, 512]) for g in range(2)] for s in range(2)]
        ps_o = [ps(f"o{n}", [P, 512]) for n in range(2)]
        ps_s, ps_d = ps("s", [P, 512]), ps("d", [P, H])

        consts, zeroed = sem("consts"), sem("zeroed")
        rkwv_loaded = [sem(f"rkwv_loaded{n}") for n in range(2)]
        g_loaded = [sem(f"g_loaded{n}") for n in range(2)]
        y_stored = sig("y_stored", 16)
        passed = sem("passed")
        d_done = sig("d_done")
        a_done = sig("a_done", 2 * LEVELS)
        nt_done = sig("nt_done", 2)
        kt_done = sig("kt_done", 2)
        s_done = sig("s_done", 2)
        o_done = sig("o_done", 2)
        p_done = sig("p_done", LEVELS)
        cp_done = sig("cp_done", 2 * LEVELS)
        r_done = sig("r_done", 2 * LEVELS)
        o_read = sig("o_read", 2)
        gn = sig("gn", 6)
        s_added = sig("s_added", 4)
        y_done = sig("y_done")
        d_copied = sig("d_copied")
        rbd_done = sig("rbd_done", 4 * LEVELS)
        sq_done = sig("sq_done")
        rooted = sig("rooted")
        yt_done = sig("yt_done", CB)
        kt_copied = sig("kt_copied", 2)
        rk_done = sig("rk_done")
        k_done = sig("k_done", 2 * LEVELS)
        dv_done = sig("dv_done")
        s_mult = sig("s_mult")
        n_done = sig("n_done")
        block = ctx.enter_context(nc.Block())

        def decay_view(parity, level):
            if level == 0:
                return wb[:, parity]
            at_col = CB * sum(CHUNK >> m for m in range(1, level))
            n = CHUNK >> level
            return decays[:, parity, at_col:at_col + CB * n].rearrange("p (b n) -> p b n", n=n)

        def halves(ap, level):
            return ap.rearrange("p b (j u q) -> p b j u q", u=2, q=1 << level)

        def by(ap, shape):
            return ap.unsqueeze(len(ap.shape)).to_broadcast(shape)

        def steps(eng, body):
            for i in (0, 1):
                body(i, 0, i)
            with eng.Fori(1, NCH // 2 - 1) as pair:
                for parity in range(2):
                    body(2 * pair + parity, pair, parity)
            for i in (NCH - 2, NCH - 1, NCH):
                body(i, i // 2, i % 2)

        def has_chunk(i):
            return not (isinstance(i, int) and i >= NCH)

        def has_next(i):
            return not (isinstance(i, int) and i + 1 >= NCH)

        def has_before(i):
            return not (isinstance(i, int) and i == 0)

        def use_of(pair, parity, of):
            return pair + (parity + of) // 2

        ORDER = ["a0", "a1", "a2", "a3", "a4", "a5", "nt", "a6", "kt"]

        def bank_set(what, parity):
            return ps_a[(ORDER.index(what) + parity) % 2]

        def wait_bank(eng, what, i, g):
            n = ORDER.index(what) - 2
            last, step = ORDER[n], (i if n >= 0 else i - 1)
            if last == "nt":
                eng.wait_ge(yt_done.sem, yt_done.now(step - 1, GB * g + GB - 1))
            elif last == "kt":
                eng.wait_ge(kt_copied.sem, kt_copied.now(step, g))
            else:
                eng.wait_ge(cp_done.sem, cp_done.now(step, 2 * int(last[1]) + g))

        @block.sync
        def _(sp):
            y_stored.grant(sp)
            sp.dma_start(ident[:], ident_dram).then_inc(consts, 16)
            sp.dma_start(masks[:], mask_dram).then_inc(consts, 16)
            sp.wait_ge(zeroed, 5)
            with nc.allow_non_contiguous_dma(reason="vectors of channels"):
                sp.dma_start(gam[:], columns(gamma)).then_inc(consts, 16)
                sp.dma_start(bet[:], columns(beta)).then_inc(consts, 16)
                u = faaaa.rearrange("(b j) n -> j n b", j=2)
                for j in range(2):
                    sp.dma_start(bonus[HEAD * j:HEAD * (j + 1), :, j], u[j]).then_inc(consts, 16)

            def load_rkwv(i, pair, parity, of):
                q = (parity + of) % 2
                cols = bass.ds((i + of) * CHUNK, CHUNK)
                for tile, src in ((rb, rT), (kb, kT), (wb, wT)):
                    sp.dma_start(tile[:, q], src[:, :, cols]).then_inc(rkwv_loaded[q], 16)
                sp.dma_start(vb[:, q], v[cols, :]).then_inc(rkwv_loaded[q], 16)

            load_rkwv(0, 0, 0, 0)

            def body(i, pair, parity):
                if has_next(i):
                    sp.wait_ge(o_done.sem, o_done.now(i - 1))
                    load_rkwv(i, pair, parity, 1)
                if has_chunk(i):
                    sp.wait_ge(y_done.sem, y_done.now(i - 2) if not isinstance(i, int) or i >= 2 else 1)
                    sp.dma_start(gb[:, parity], gT[:, :, bass.ds(i * CHUNK, CHUNK)]).then_inc(g_loaded[parity], 16)
                if has_before(i):
                    sp.wait_ge(y_done.sem, y_done.now(i - 1))
                    sp.dma_start(yT[:, :, bass.ds((i - 1) * CHUNK, CHUNK)], yb[:]).then_inc(y_stored.sem, 16)

            steps(sp, body)
            sp.wait_ge(y_stored.sem, y_stored.now(NCH - 1))

        @block.gpsimd
        def _(pool):
            for s in (rk_done, k_done, dv_done, s_mult, n_done):
                s.grant(pool)
            pool.memset(at[:], 0.0).then_inc(zeroed, 1)

            def products(i, pair, parity, of):
                q = (parity + of) % 2
                pool.wait_ge(rkwv_loaded[q], 64 * (use_of(pair, parity, of) + 1))
                pool.wait_ge(d_done.sem, d_done.now(i + of - 1))
                pool.tensor_tensor(rk[:], rb[:, q], kb[:, q], ALU.mult).then_inc(rk_done.sem, 1)

            products(0, 0, 0, 0)

            def body(i, pair, parity):
                if not has_chunk(i):
                    normed(i)
                    return
                for l in range(LEVELS):
                    for g in range(2):
                        pool.wait_ge(a_done.sem, a_done.now(i, 2 * l + g))
                        if l == 0:
                            pool.wait_ge(rk_done.sem, rk_done.now(i))
                        else:
                            pool.wait_ge(p_done.sem, p_done.now(i, l - 1))
                            pool.wait_ge(k_done.sem, k_done.now(i, 2 * (l - 1) + g))
                        blocks = slice(GB * g, GB * g + GB)
                        left = halves(kb[:, parity, blocks, :], l)[:, :, :, 0, :]
                        right_decay = decay_view(parity, l)[:, blocks, 1::2]
                        pool.tensor_tensor(left, left, by(right_decay, left.shape),
                                           ALU.mult).then_inc(k_done.sem, 1)
                    if l == 1:
                        pool.wait_ge(o_read.sem, o_read.now(i - 1))
                        pool.wait_ge(d_copied.sem, d_copied.now(i))
                        heads = lambda ap: ap.rearrange("p (h m) -> p h m", m=HEAD)
                        pool.tensor_tensor(heads(dv[:]), heads(vb[:, parity]), by(dsb[:], [P, H, HEAD]),
                                           ALU.mult).then_inc(dv_done.sem, 1)
                    if l == 4:
                        normed(i)
                    if l == 5 and has_next(i):
                        products(i, pair, parity, 1)
                pool.wait_ge(s_added.sem, s_added.now(i - 1))
                pool.wait_ge(o_done.sem, o_done.now(i - 1))
                pool.wait_ge(p_done.sem, p_done.now(i))
                pool.tensor_tensor(state[:, 1 - parity], state[:, parity],
                                   decay_view(parity, LEVELS).to_broadcast([P, CB, P]),
                                   ALU.mult).then_inc(s_mult.sem, 1)

            def normed(i):
                if not has_before(i):
                    return
                pool.wait_ge(gn.sem, gn.now(i - 1, 5))
                pool.wait_ge(nt_done.sem, nt_done.now(i - 2) if not isinstance(i, int) or i >= 2 else 2)
                heads = lambda ap: ap.rearrange("p (h m) -> p h m", m=HEAD)
                pool.tensor_tensor(heads(nrm[:]), heads(cen[:]), by(grs[:], [P, H, HEAD]),
                                   ALU.mult).then_inc(n_done.sem, 1)

            steps(pool, body)

        @block.vector
        def _(dve):
            for s in (p_done, cp_done, r_done, o_read, gn, s_added, y_done):
                s.grant(dve)
            for tile in (rbd, state, bonus):
                dve.memset(tile[:], 0.0).then_inc(zeroed, 1)
            dve.memset(dsb[:], 0.0).then_inc(zeroed, 1)
            dve.wait_ge(consts, 16 * 6)
            dve.wait_ge(zeroed, 5)

            def block_decays(i, pair, parity, of):
                q = (parity + of) % 2
                dve.wait_ge(rkwv_loaded[q], 64 * (use_of(pair, parity, of) + 1))
                dve.wait_ge(s_mult.sem, s_mult.now(i + of - 2) if not isinstance(i, int) or i + of >= 2 else 1)
                dve.wait_ge(r_done.sem, r_done.now(i + of - 1))
                for l in range(LEVELS):
                    if l:
                        dve.wait_ge(p_done.sem, p_done.now(i + of, l - 1))
                    src = decay_view(q, l)
                    dve.tensor_tensor(decay_view(q, l + 1), src[:, :, 0::2], src[:, :, 1::2],
                                      ALU.mult).then_inc(p_done.sem, 1)

            block_decays(0, 0, 0, 0)

            def body(i, pair, parity):
                b = i - 1
                if not has_chunk(i):
                    norm_a(i)
                    norm_b(i)
                    norm_c(i)
                    norm_d(i)
                    gate(i, pair, parity)
                    return
                if not isinstance(i, int) or i >= 2:
                    dve.wait_ge(o_done.sem, o_done.now(i - 2))
                for l in range(LEVELS):
                    for g in range(2):
                        blocks = slice(GB * g, GB * g + GB)
                        dve.wait_ge(a_done.sem, a_done.now(i, 2 * l + g))
                        if l:
                            dve.wait_ge(cp_done.sem, cp_done.now(i, 2 * (l - 1) + g))
                        hop(dve, passed)
                        dst = halves(at[:, parity, H // 2 * g:H // 2 * (g + 1), :], l)[:, :, :, 1, :]
                        n = HALF >> l
                        msk = masks[:, l, :].rearrange("p (j q) -> p j q", j=n).unsqueeze(1)
                        src = bank_set(f"a{l}", parity)[g][:].rearrange("p (h j q) -> p h j q", h=H // 2, j=n)
                        dve.copy_predicated(dst, msk.to_broadcast(dst.shape), src).then_inc(cp_done.sem, 1)
                        dve.wait_ge(rbd_done.sem, rbd_done.now(i, 4 * l + 2 * g + 1))
                        if l == 0:
                            dve.wait_ge(rk_done.sem, rk_done.now(i))
                        else:
                            dve.wait_ge(p_done.sem, p_done.now(i, l - 1))
                            dve.wait_ge(r_done.sem, r_done.now(i, 2 * (l - 1) + g))
                        right = halves(rb[:, parity, blocks, :], l)[:, :, :, 1, :]
                        left_decay = decay_view(parity, l)[:, blocks, 0::2]
                        dve.tensor_tensor(right, right, by(left_decay, right.shape),
                                          ALU.mult).then_inc(r_done.sem, 1)
                    if has_before(i):
                        if l == 0:
                            norm_a(i)
                        if l == 1:
                            norm_b(i)
                        if l == 3:
                            norm_c(i)
                        if l == 4:
                            norm_d(i)
                if has_next(i):
                    block_decays(i, pair, parity, 1)
                if has_before(i):
                    gate(i, pair, parity)
                for n in range(2):
                    dve.wait_ge(s_done.sem, s_done.now(i, n))
                    if n == 0:
                        dve.wait_ge(s_mult.sem, s_mult.now(i))
                    for j in range(2):
                        rows = slice(HEAD * j, HEAD * j + HEAD)
                        own = state[rows, 1 - parity, GB * n:GB * n + GB, rows]
                        got = ps_s[rows, :].rearrange("p (b m) -> p b m", m=P)[:, :, rows]
                        dve.tensor_tensor(own, own, got, ALU.add).then_inc(s_added.sem, 1)

            def norm_a(i):
                for n in range(2):
                    cols = slice(512 * n, 512 * n + 512)
                    dve.wait_ge(o_done.sem, o_done.now(i - 1, n))
                    dve.wait_ge(dv_done.sem, dv_done.now(i - 1))
                    dve.wait_ge(gn.sem, gn.now(i - 1, 2) - 6)
                    dve.tensor_tensor(ob[:, cols], ps_o[n][:], dv[:, cols], ALU.add).then_inc(o_read.sem, 1)

            def norm_b(i):
                heads = lambda ap: ap.rearrange("p (h m) -> p h m", m=HEAD)
                dve.wait_ge(o_read.sem, o_read.now(i - 1))
                dve.tensor_reduce(gsum[:], heads(ob[:]), AX_X, ALU.add).then_inc(gn.sem, 1)
                dve.wait_ge(gn.sem, gn.now(i - 1, 0))
                dve.tensor_scalar(gmean[:], gsum[:], 1.0 / HEAD, None, ALU.mult).then_inc(gn.sem, 1)
                dve.wait_ge(gn.sem, gn.now(i - 1, 1))
                dve.wait_ge(n_done.sem, n_done.now(i - 1) - 1)
                dve.tensor_tensor(heads(cen[:]), heads(ob[:]), by(gmean[:], [P, H, HEAD]),
                                  ALU.subtract).then_inc(gn.sem, 1)

            def norm_c(i):
                dve.wait_ge(sq_done.sem, sq_done.now(i - 1))
                dve.tensor_reduce(gvar[:], sq[:].rearrange("p (h m) -> p h m", m=HEAD), AX_X,
                                  ALU.add).then_inc(gn.sem, 1)
                dve.wait_ge(gn.sem, gn.now(i - 1, 3))
                dve.tensor_scalar(gve[:], gvar[:], 1.0 / HEAD, GN_EPS, ALU.mult, ALU.add).then_inc(gn.sem, 1)

            def norm_d(i):
                dve.wait_ge(rooted.sem, rooted.now(i - 1))
                dve.reciprocal(grs[:], gsd[:]).then_inc(gn.sem, 1)

            def gate(i, pair, parity):
                q = 1 - parity
                dve.wait_ge(yt_done.sem, yt_done.now(i - 1))
                dve.wait_ge(g_loaded[q], 16 * (use_of(pair, parity, -1) + 1))
                dve.wait_ge(y_stored.sem, y_stored.now(i - 2))
                dve.tensor_tensor(yb[:], yt[:], gb[:, q], ALU.mult).then_inc(y_done.sem, 1)

            steps(dve, body)

        @block.scalar
        def _(act):
            for s in (d_copied, rbd_done, sq_done, rooted, yt_done, kt_copied):
                s.grant(act)
            act.wait_ge(consts, 16 * 6)
            act.wait_ge(zeroed, 5)

            def body(i, pair, parity):
                if has_chunk(i):
                    act.wait_ge(rkwv_loaded[parity], 64 * (use_of(pair, parity, 0) + 1))
                for l in range(LEVELS):
                    for g in range(2 if has_chunk(i) else 0):
                        if l:
                            act.wait_ge(r_done.sem, r_done.now(i, 2 * (l - 1) + g))
                        if l >= 2:
                            act.wait_ge(a_done.sem, a_done.now(i, 2 * (l - 2) + g))
                        else:
                            act.wait_ge(a_done.sem, a_done.now(i - 1, 2 * (6 - l) + g))
                        for j in range(2):
                            rows = slice(HEAD * j, HEAD * j + HEAD)
                            right = halves(rb[rows, parity, GB * g:GB * g + GB, :], l)[:, :, :, 1, :]
                            dst = rbd[rows, l % 2, GB * g:GB * g + GB, HALF * j:HALF * j + HALF]
                            act.copy(dst.rearrange("p b (j q) -> p b j q", q=1 << l),
                                     right).then_inc(rbd_done.sem, 1)
                    if l == 0 and has_chunk(i):
                        act.wait_ge(d_done.sem, d_done.now(i))
                        act.wait_ge(dv_done.sem, dv_done.now(i - 1))
                        act.copy(dsb[:], ps_d[:]).then_inc(d_copied.sem, 1)
                    if has_before(i):
                        if l == 2:
                            act.wait_ge(gn.sem, gn.now(i - 1, 2))
                            act.activation(sq[:], cen[:], ACT.Square).then_inc(sq_done.sem, 1)
                        if l == 4:
                            act.wait_ge(gn.sem, gn.now(i - 1, 4))
                            act.activation(gsd[:], gve[:], ACT.Sqrt).then_inc(rooted.sem, 1)
                if has_before(i):
                    for b in range(CB):
                        act.wait_ge(nt_done.sem, nt_done.now(i - 1, b // GB))
                        act.wait_ge(y_done.sem, y_done.now(i - 1) - 1)
                        bank = bank_set("nt", parity)[b // GB]
                        act.activation(yt[:, b, :], bank[:, (b % GB) * P:(b % GB + 1) * P], ACT.Identity,
                                       bias=bet[:, b:b + 1], scale=gam[:, b:b + 1]).then_inc(yt_done.sem, 1)
                for g in range(2 if has_chunk(i) else 0):
                    act.wait_ge(kt_done.sem, kt_done.now(i, g))
                    act.wait_ge(s_done.sem, s_done.now(i - 1, g))
                    act.copy(kt[:, 512 * g:512 * g + 512], bank_set("kt", parity)[g][:]).then_inc(kt_copied.sem, 1)

            steps(act, body)

        @block.tensor
        def _(pe):
            for s in (d_done, a_done, nt_done, kt_done, s_done, o_done):
                s.grant(pe)
            pe.wait_ge(consts, 16 * 6)
            pe.wait_ge(zeroed, 5)

            def body(i, pair, parity):
                if has_chunk(i):
                    pe.wait_ge(rk_done.sem, rk_done.now(i))
                    pe.wait_ge(d_copied.sem, d_copied.now(i - 1))
                    for b in range(CB):
                        mm = pe.matmul(ps_d[:, 2 * b:2 * b + 2], rk[:, b, :], bonus[:, b, :], start=True, stop=True)
                    mm.then_inc(d_done.sem, 1)
                for what in ORDER:
                    if what == "nt":
                        if has_before(i):
                            turn_norm(i, parity)
                        continue
                    if not has_chunk(i) or what == "kt":
                        continue
                    l = int(what[1])
                    for g in range(2):
                        wait_bank(pe, what, i, g)
                        pe.wait_ge(rbd_done.sem, rbd_done.now(i, 4 * l + 2 * g + 1))
                        if l:
                            pe.wait_ge(k_done.sem, k_done.now(i, 2 * (l - 1) + g))
                        for b in range(GB * g, GB * g + GB):
                            mm = pe.matmul(bank_set(what, parity)[g][:, (b % GB) * P:(b % GB + 1) * P],
                                           kb[:, parity, b, :], rbd[:, l % 2, b, :], start=True, stop=True)
                        mm.then_inc(a_done.sem, 1)
                if has_chunk(i):
                    outputs(i, parity)

            def turn_norm(i, parity):
                pe.wait_ge(n_done.sem, n_done.now(i - 1))
                for g in range(2):
                    if has_chunk(i):
                        wait_bank(pe, "nt", i, g)
                    else:
                        pe.wait_ge(cp_done.sem, cp_done.now(i - 1))
                        pe.wait_ge(kt_copied.sem, kt_copied.now(i - 1))
                    for b in range(GB * g, GB * g + GB):
                        mm = pe.transpose(bank_set("nt", parity)[g][:, (b % GB) * P:(b % GB + 1) * P],
                                          nrm[:, b * P:(b + 1) * P], ident[:])
                    mm.then_inc(nt_done.sem, 1)

            def outputs(i, parity):
                for g in range(2):
                    wait_bank(pe, "kt", i, g)
                    pe.wait_ge(k_done.sem, k_done.now(i, 2 * (LEVELS - 1) + g))
                    for b in range(GB * g, GB * g + GB):
                        mm = pe.transpose(bank_set("kt", parity)[g][:, (b % GB) * P:(b % GB + 1) * P],
                                          kb[:, parity, b, :], ident[:])
                    mm.then_inc(kt_done.sem, 1)
                for n in range(2):
                    pe.wait_ge(kt_copied.sem, kt_copied.now(i, n))
                    if n == 0:
                        pe.wait_ge(s_added.sem, s_added.now(i - 1))
                    else:
                        pe.wait_ge(s_added.sem, s_added.now(i, 1))
                    for b in range(GB * n, GB * n + GB):
                        cols = slice(b * P, b * P + P)
                        mm = pe.matmul(ps_s[:, (b % GB) * P:(b % GB + 1) * P], kt[:, cols], vb[:, parity, cols],
                                       start=True, stop=True)
                    mm.then_inc(s_done.sem, 1)
                    pe.wait_ge(o_read.sem, o_read.now(i - 1, n))
                    pe.wait_ge(r_done.sem, r_done.now(i))
                    pe.wait_ge(cp_done.sem, cp_done.now(i))
                    for b in range(GB * n, GB * n + GB):
                        at_col = (b % GB) * P
                        pe.matmul(ps_o[n][:, at_col:at_col + P], rb[:, parity, b, :], state[:, parity, b, :],
                                  start=True, stop=False)
                        for j in range(2):
                            head = 2 * b + j
                            mm = pe.matmul(ps_o[n][:, at_col + HEAD * j:at_col + HEAD * j + HEAD],
                                           at[:, parity, head, :], vb[:, parity, head * HEAD:(head + 1) * HEAD],
                                           start=False, stop=j == 1)
                    mm.then_inc(o_done.sem, 1)

            steps(pe, body)


def level_masks():
    import numpy as np

    s = np.arange(CHUNK)[:, None]
    masks = []
    for level in range(LEVELS):
        size = 1 << level
        t = np.arange(CHUNK).reshape(-1, 2, size)[:, 1].reshape(1, -1)
        masks.append((s // (2 * size) == t // (2 * size)) & (s // size % 2 == 0))
    return np.ascontiguousarray(np.stack(masks, 1).astype(np.int32))


def output_phase(nc, yT, x, w_o, factors_sum, bias, ident_dram, out):
    with ExitStack() as ctx:
        sb = lambda name, shape, dt=F32: ctx.enter_context(nc.sbuf_tensor("o_" + name, shape, dt))
        ps = lambda name: ctx.enter_context(nc.psum_tensor("o_" + name, [P, 512], F32))
        phase = ctx.enter_context(Phase(nc, "o_"))
        sig, sem = phase.counter, phase.semaphore
        NT = T // P
        GB = CB // 2
        wo_hi, wo_lo, wf_hi, wf_lo = (sb(n, [P, CB, C], F32R) for n in ("wohi", "wolo", "wfhi", "wflo"))
        split_load, split_high, split_low, (w_low, n_low) = load_split(
            nc, ctx, phase, [(w_o, wo_hi, wo_lo), (factors_sum, wf_hi, wf_lo)])
        ident = sb("ident", [P, P])
        brow = sb("brow", [P, C])
        yb = sb("yb", [P, CB, P])
        y_hi, y_lo = sb("yhi", [P, 2, CB, P], F32R), sb("ylo", [P, 2, CB, P], F32R)
        xb = sb("xb", [P, C])
        x1 = sb("x1", [P, C])
        x1b = sb("x1b", [P, 2, C])
        stats, mv = sb("stats", [P, 12]), sb("mv", [P, 2])
        eps, sd, rstd, nmr = (sb(n, [P, 1]) for n in ("eps", "sd", "rstd", "nmr"))
        h2 = sb("h2", [P, C])
        h_hi, h_lo = sb("hhi", [P, CB, P], F32R), sb("hlo", [P, CB, P], F32R)
        fin = sb("fin", [P, C])
        ps_o, ps_f, ps_t = ([ps(f"{n}{g}") for g in range(2)] for n in "oft")

        consts, zeroed, passed = sem("consts"), sem("zeroed"), sem("passed")
        y_loaded, x_loaded = sem("y_loaded"), sem("x_loaded")
        stored = sig("stored", 16)
        o_done, f_done, t_done = sig("o_done", 2), sig("f_done", 2), sig("t_done", 2)
        ylo_done, x1_done, stat, aggr = sig("ylo_done"), sig("x1_done", 2), sig("stat", 2), sig("aggr")
        scaled, hlo_done, fin_done = sig("scaled", 2), sig("hlo_done", 2), sig("fin_done", 2)
        yhi_done, rooted, h2_done, hhi_done = sig("yhi_done"), sig("rooted"), sig("h2_done"), sig("hhi_done", 2)
        x1b_done = sig("x1b_done")
        block = ctx.enter_context(nc.Block())

        def steps(eng, body):
            for i in (0, 1):
                body(i, i)
            with eng.Fori(1, NT // 2 - 1) as pair:
                for parity in range(2):
                    body(2 * pair + parity, parity)
            for i in range(NT - 2, NT + 2):
                body(i, i % 2)

        def has(i, back):
            return not isinstance(i, int) or 0 <= i - back < NT

        def old(signal, i, back, k=None):
            if isinstance(i, int) and i - back < -1:
                return signal.now(-1)
            return signal.now(i - back, k)

        @block.sync
        def _(sp):
            stored.grant(sp)
            sp.dma_start(ident[:], ident_dram).then_inc(consts, 16)
            sp.dma_start(brow[:], bias.rearrange("(a n) -> a n", a=1).to_broadcast([P, C])).then_inc(consts, 16)

            def load_y(i):
                sp.wait_ge(ylo_done.sem, old(ylo_done, i, 1))
                sp.dma_start(yb[:], yT[:, :, bass.ds(i * P, P)]).then_inc(y_loaded, 16)

            load_y(0)
            split_load(sp)

            def body(i, parity):
                if has(i, -1):
                    load_y(i + 1)
                if has(i, 0):
                    sp.wait_ge(x1_done.sem, old(x1_done, i, 1))
                    sp.dma_start(xb[:], x[bass.ds(i * P, P), :]).then_inc(x_loaded, 16)
                if has(i, 2):
                    sp.wait_ge(fin_done.sem, fin_done.now(i - 2))
                    sp.dma_start(out[bass.ds((i - 2) * P, P), :], fin[:]).then_inc(stored.sem, 16)

            steps(sp, body)
            sp.wait_ge(stored.sem, stored.now(NT - 1))

        @block.gpsimd
        def _(pool):
            x1b_done.grant(pool)
            pool.wait_ge(consts, 32)

            def body(i, parity):
                if has(i, 0):
                    pool.wait_ge(x1_done.sem, x1_done.now(i))
                    pool.wait_ge(fin_done.sem, old(fin_done, i, 2))
                    pool.tensor_tensor(x1b[:, parity], x1[:], brow[:], ALU.add).then_inc(x1b_done.sem, 1)

            steps(pool, body)

        @block.vector
        def _(dve):
            for s in (ylo_done, x1_done, stat, aggr, scaled, hlo_done, fin_done):
                s.grant(dve)
            dve.memset(eps[:], LN_EPS).then_inc(zeroed, 1)

            def y_low(i, parity):
                dve.wait_ge(yhi_done.sem, yhi_done.now(i))
                dve.tensor_tensor(y_lo[:, parity], yb[:], y_hi[:, parity].bitcast(F32),
                                  ALU.subtract).then_inc(ylo_done.sem, 1)

            y_low(0, 0)
            split_low(dve)

            def body(i, parity):
                if has(i, 1):
                    for g in range(2):
                        dve.wait_ge(hhi_done.sem, hhi_done.now(i - 1, g))
                        blocks = slice(GB * g, GB * g + GB)
                        dve.tensor_tensor(h_lo[:, blocks], ps_t[g][:].rearrange("p (b t) -> p b t", b=GB),
                                          h_hi[:, blocks].bitcast(F32), ALU.subtract).then_inc(hlo_done.sem, 1)

            def main(i, parity):
                if has(i, -1):
                    y_low(i + 1, 1 - parity)
                if has(i, 0):
                    dve.wait_ge(h2_done.sem, old(h2_done, i, 1))
                    dve.wait_ge(x1b_done.sem, old(x1b_done, i, 1))
                    dve.wait_ge(x_loaded, 16 * (i + 1))
                    for g in range(2):
                        cols = slice(512 * g, 512 * g + 512)
                        dve.wait_ge(o_done.sem, o_done.now(i, g))
                        dve.tensor_tensor(x1[:, cols], ps_o[g][:], xb[:, cols], ALU.add).then_inc(x1_done.sem, 1)
                    dve.wait_ge(aggr.sem, old(aggr, i, 1))
                    for g in range(2):
                        dve.wait_ge(x1_done.sem, x1_done.now(i, g))
                        dve.bn_stats(stats[:, 6 * g:6 * g + 6], x1[:, 512 * g:512 * g + 512]).then_inc(stat.sem, 1)
                    dve.wait_ge(stat.sem, stat.now(i))
                    dve.wait_ge(scaled.sem, old(scaled, i, 1))
                    hop(dve, passed)
                    dve.bn_aggr(mv[:], stats[:]).then_inc(aggr.sem, 1)
                    dve.wait_ge(rooted.sem, rooted.now(i))
                    dve.reciprocal(rstd[:], sd[:]).then_inc(scaled.sem, 1)
                    dve.wait_ge(scaled.sem, scaled.now(i, 0))
                    dve.scalar_tensor_tensor(nmr[:], mv[:, 0:1], -1.0, rstd[:], ALU.mult,
                                             ALU.mult).then_inc(scaled.sem, 1)
                if has(i, 2):
                    dve.wait_ge(x1b_done.sem, x1b_done.now(i - 2))
                    dve.wait_ge(stored.sem, stored.now(i - 3))
                    for g in range(2):
                        cols = slice(512 * g, 512 * g + 512)
                        dve.wait_ge(f_done.sem, f_done.now(i - 2, g))
                        dve.scalar_tensor_tensor(fin[:, cols], ps_f[g][:], float(RANK) ** -0.5, x1b[:, parity, cols],
                                                 ALU.mult, ALU.add).then_inc(fin_done.sem, 1)
                body(i, parity)

            steps(dve, main)

        @block.scalar
        def _(act):
            for s in (yhi_done, rooted, h2_done, hhi_done):
                s.grant(act)
            act.wait_ge(zeroed, 1)

            def y_high(i, parity):
                act.wait_ge(y_loaded, 16 * (i + 1))
                act.wait_ge(o_done.sem, old(o_done, i, 2))
                act.copy(y_hi[:, parity], yb[:]).then_inc(yhi_done.sem, 1)

            y_high(0, 0)
            split_high(act)

            def body(i, parity):
                if has(i, -1):
                    y_high(i + 1, 1 - parity)
                if has(i, 0):
                    act.wait_ge(aggr.sem, aggr.now(i))
                    act.activation(sd[:], mv[:, 1:2], ACT.Sqrt, bias=eps[:]).then_inc(rooted.sem, 1)
                    act.wait_ge(scaled.sem, scaled.now(i))
                if has(i, 1):
                    for g in range(2):
                        act.wait_ge(t_done.sem, t_done.now(i - 1, g))
                        act.wait_ge(f_done.sem, old(f_done, i, 2))
                        act.copy(h_hi[:, GB * g:GB * g + GB], ps_t[g][:].rearrange("p (b t) -> p b t", b=GB)
                                 ).then_inc(hhi_done.sem, 1)
                if has(i, 0):
                    act.wait_ge(t_done.sem, old(t_done, i, 1))
                    act.activation(h2[:], x1[:], ACT.Identity, bias=nmr[:], scale=rstd[:]).then_inc(h2_done.sem, 1)

            steps(act, body)

        @block.tensor
        def _(pe):
            for s in (o_done, f_done, t_done):
                s.grant(pe)
            pe.wait_ge(consts, 32)

            def product(banks, left_hi, left_lo, right_hi, right_lo, done):
                for g in range(2):
                    cols = slice(512 * g, 512 * g + 512)
                    for b in range(CB):
                        pe.matmul(banks[g][:], left_hi[:, b, :], right_hi[:, b, cols], start=b == 0, stop=False)
                        pe.matmul(banks[g][:], left_hi[:, b, :], right_lo[:, b, cols], start=False, stop=False)
                        mm = pe.matmul(banks[g][:], left_lo[:, b, :], right_hi[:, b, cols], start=False,
                                       stop=b == CB - 1)
                    mm.then_inc(done.sem, 1)

            pe.wait_ge(w_low, n_low)

            def body(i, parity):
                if has(i, 0):
                    pe.wait_ge(ylo_done.sem, ylo_done.now(i))
                    pe.wait_ge(x1_done.sem, old(x1_done, i, 1))
                    product(ps_o, y_hi[:, parity], y_lo[:, parity], wo_hi, wo_lo, o_done)
                if has(i, 2):
                    pe.wait_ge(hlo_done.sem, hlo_done.now(i - 2))
                    pe.wait_ge(fin_done.sem, old(fin_done, i, 3))
                    product(ps_f, h_hi, h_lo, wf_hi, wf_lo, f_done)
                if has(i, 1):
                    pe.wait_ge(h2_done.sem, h2_done.now(i - 1))
                    for g in range(2):
                        pe.wait_ge(hlo_done.sem, old(hlo_done, i, 2, g))
                        for b in range(GB * g, GB * g + GB):
                            mm = pe.transpose(ps_t[g][:, (b % GB) * P:(b % GB + 1) * P], h2[:, b * P:(b + 1) * P],
                                              ident[:])
                        mm.then_inc(t_done.sem, 1)

            steps(pe, body)


def build(nc, a, out):
    def scratch(name, shape):
        return nc.dram_tensor(name, shape, F32, kind="Internal").ap()

    blocks = lambda ap: ap.rearrange("(b p) n -> p b n", p=P)
    hT, zs = blocks(scratch("hT", [C, T + 1])), scratch("zs", [NMIX, 3 * DMIX, T])
    factors_sum = scratch("factors_sum", [C, C])
    rT, kT, gT, wT, yT = (blocks(scratch(n, [C, T])) for n in ("rT", "kT", "gT", "wT", "yT"))
    v = scratch("v", [T, C])
    norm_phase(nc, a["hidden"], a["time_maa_x"], a["time_maa_w1"], a["ident"], a["factors"], hT, zs, factors_sum)
    for n, (kind, what, dst) in enumerate((("w", "w", wT), ("rk", "k", kT), ("v", "v", v), ("rk", "r", rT),
                                           ("g", "g", gT))):
        decay = (a["time_decay_w1"], a["time_decay_w2"], a["time_decay"]) if kind == "w" else None
        weight = None if kind == "w" else blocks(a["W_" + what])
        projection_phase(nc, kind, hT, zs[n], a["time_maa_" + what], a["time_maa_w2"][n], dst, weight, decay)
    recurrence_phase(nc, rT, kT, wT, gT, v, a["time_faaaa"], a["ln_gamma"], a["ln_beta"], a["ident"], a["masks"], yT)
    output_phase(nc, yT, a["hidden"], blocks(a["W_o"]), blocks(factors_sum), a["bias"], a["ident"], out)


def kernel(**inputs):
    import numpy as np
    import concourse.bacc as bacc
    from concourse.bass_utils import run_bass_kernel_spmd

    given = {}
    for name, value in inputs.items():
        short = name.removeprefix("L0_attn_").removeprefix("L0_ffn_")
        value = np.asarray(value)
        if short.startswith("W_"):
            value = value.T
        elif short == "hidden":
            value = value[0]
        elif short.startswith("time_maa_") and value.ndim == 3 and value.shape[0] == 1 or short == "time_decay":
            value = value.reshape(-1)
        given[short] = np.ascontiguousarray(value)
    given["ident"] = np.eye(P, dtype=np.float32)
    given["masks"] = level_masks()

    nc = bacc.Bacc("TRN2", target_bir_lowering=False, num_devices=1)
    arrays, aps = {}, {}
    for name, value in given.items():
        arrays[f"in_{name}"] = value
        aps[name] = nc.dram_tensor(f"in_{name}", value.shape, mybir.dt.from_np(value.dtype), kind="ExternalInput").ap()
    out = nc.dram_tensor("out", [T, C], F32, kind="ExternalOutput").ap()
    build(nc, aps, out)
    results = run_bass_kernel_spmd(nc, [arrays], core_ids=[0])
    return results.results[0]["out"].reshape(1, T, C)
```

```python
from contextlib import ExitStack

import concourse.bass as bass
from concourse import mybir

F32 = mybir.dt.float32
F32R = mybir.dt.float32r
I32 = mybir.dt.int32
ALU = mybir.AluOpType
ACT = mybir.ActivationFunctionType
AX_X = mybir.AxisListType.X

P = 128
C = 1024
T = 4096
HEAD = 64
H = C // HEAD
CB = C // P
DMIX = 32
NMIX = 5
DDEC = 64
RANK = 8
WIN = 512
NW = T // WIN
SUB = WIN // P
LN_EPS = 1e-5
GN_EPS = 1e-5 * 8.0 ** 2
CHUNK = 128
NCH = T // CHUNK
LEVELS = 7


class Phase:

    def __init__(self, nc, prefix):
        self.nc, self.prefix, self.held = nc, prefix, []

    def __enter__(self):
        return self

    def semaphore(self, name):
        self.held.append(self.nc.alloc_semaphore(self.prefix + name))
        return self.held[-1]

    def counter(self, name, per=1):
        return Counter(self.semaphore(name), per)

    def __exit__(self, *error):
        if error[0] is None:
            self.nc.clear_and_free_semaphores(self.held)
            self.nc.all_engine_barrier()


class Counter:

    def __init__(self, sem, per=1):
        self.sem, self.per = sem, per

    def grant(self, eng):
        eng.sem_inc(self.sem, self.per)

    def now(self, step, k=None):
        return self.per * (step + 1) + (self.per if k is None else k + 1)

    def prev(self, step, k=None):
        return self.per * step + (self.per if k is None else k + 1)


def columns(vector_dram):
    return vector_dram.rearrange("(b p) -> p b", p=P)


def hop(eng, passed):
    eng.sem_inc(passed, 1)


def norm_phase(nc, x, maa_x, w1, ident_dram, hT, zs):
    with ExitStack() as ctx:
        sb = lambda name, shape, dt=F32: ctx.enter_context(nc.sbuf_tensor(name, shape, dt))
        phase = ctx.enter_context(Phase(nc, "n_"))
        sig, sem = phase.counter, phase.semaphore
        ident = sb("n_ident", [P, P])
        maa = sb("n_maa", [P, CB])
        w1s = sb("n_w1", [P, CB, NMIX * DMIX])
        xb = sb("n_x", [P, 2, SUB, C])
        stats = sb("n_stats", [P, SUB, 12])
        mv = sb("n_mv", [P, SUB, 2])
        sd = sb("n_sd", [P, SUB])
        rstd = sb("n_rstd", [P, SUB])
        nmr = sb("n_nmr", [P, SUB])
        eps = sb("n_eps", [P, 1])
        xn = sb("n_xn", [P, SUB, C])
        h = sb("n_h", [P, CB, WIN + 1])
        zero = sb("n_zero", [P, CB])
        xx = sb("n_xx", [P, 2, WIN])
        xxx = sb("n_xxx", [P, 4, WIN])
        za, zb = sb("n_za", [P, WIN]), sb("n_zb", [DMIX, WIN])
        za_hi, zb_hi = sb("n_zahi", [P, WIN], F32R), sb("n_zbhi", [DMIX, WIN], F32R)
        za_lo, zb_lo = sb("n_zalo", [P, WIN], F32R), sb("n_zblo", [DMIX, WIN], F32R)
        ps_t = [ctx.enter_context(nc.psum_tensor(f"n_pst{b}", [P, WIN], F32)) for b in range(4)]
        ps_za = ctx.enter_context(nc.psum_tensor("n_psza", [P, WIN], F32))
        ps_zb = ctx.enter_context(nc.psum_tensor("n_pszb", [DMIX, WIN], F32))

        consts, zero_stored, zeroed = sem("consts"), sem("zero_stored"), sem("zeroed")
        x_loaded = [[sem(f"x_loaded{q}{j}") for j in range(SUB)] for q in range(2)]
        h_stored = [sig(f"h_stored{b}", 16) for b in range(CB)]
        z_stored = sig("z_stored", 16 * 6)
        passed, pool_passed = sem("passed"), sem("pool_passed")
        stat = sig("stat", 2 * SUB)
        aggr = sig("aggr", SUB)
        rooted = sig("rooted")
        scaled = sig("scaled", 2)
        xn_ready = sig("xn_ready", SUB)
        turned = sig("turned", CB)
        h_ready = sig("h_ready", CB)
        xx_ready = sig("xx_ready", CB)
        carried = sig("carried", CB)
        xxx_ready = sig("xxx_ready", CB)
        z_step = sig("z_step", CB)
        z_tanh = sig("z_tanh", 2)
        z_hi = sig("z_hi", 2)
        z_lo = sig("z_lo", 2)
        block = ctx.enter_context(nc.Block())

        def windows(eng, body):
            body(0, 0, 0)
            body(1, 0, 1)
            with eng.Fori(1, NW // 2 - 1) as pair:
                for parity in range(2):
                    body(2 * pair + parity, pair, parity)
            body(NW - 2, NW // 2 - 1, 0)
            body(NW - 1, NW // 2 - 1, 1)

        @block.sync
        def _(sp):
            sp.dma_start(ident[:], ident_dram).then_inc(consts, 16)
            with nc.allow_non_contiguous_dma(reason="one vector of channels"):
                sp.dma_start(maa[:], columns(maa_x)).then_inc(consts, 16)
            sp.dma_start(w1s[:], w1.rearrange("(b p) d -> p b d", p=P)).then_inc(consts, 16)
            sp.wait_ge(zeroed, 3)
            with nc.allow_non_contiguous_dma(reason="the zero token in front"):
                sp.dma_start(hT[:, :, 0], zero[:]).then_inc(zero_stored, 16)

            def load_x(w, parity):
                for j in range(SUB):
                    if not isinstance(w, int) or w >= 2:
                        sp.wait_ge(xn_ready.sem, xn_ready.prev(w, j) - SUB)
                    sp.dma_start(xb[:, parity, j, :], x[bass.ds(w * WIN + j * P, P), :]
                                 ).then_inc(x_loaded[parity][j], 16)

            load_x(0, 0)
            load_x(1, 1)
            with sp.Fori(1, NW // 2) as pair:
                for parity in range(2):
                    load_x(2 * pair + parity, parity)

        @block.gpsimd
        def _(pool):
            carried.grant(pool)

            with pool.Fori(0, NW) as w:
                for b in range(CB):
                    pool.wait_ge(xx_ready.sem, xx_ready.now(w, b))
                    hop(pool, pool_passed)
                    pool.tensor_copy(h[:, b, 0:1], h[:, b, WIN:WIN + 1]).then_inc(carried.sem, 1)

        @block.vector
        def _(dve):
            dve.memset(h[:], 0.0).then_inc(zeroed, 1)
            dve.memset(zero[:], 0.0).then_inc(zeroed, 1)
            dve.memset(eps[:], LN_EPS).then_inc(zeroed, 1)
            for s in (stat, aggr, scaled, xx_ready, xxx_ready, z_lo):
                s.grant(dve)
            dve.wait_ge(consts, 48)

            def statistics(w, use, q):
                for j in range(SUB):
                    dve.wait_ge(x_loaded[q][j], 16 * (use + 1))
                    if j == 0:
                        dve.wait_ge(aggr.sem, aggr.prev(w))
                    for half in range(2):
                        dve.bn_stats(stats[:, j, 6 * half:6 * half + 6],
                                     xb[:, q, j, 512 * half:512 * half + 512]).then_inc(stat.sem, 1)
                dve.wait_ge(scaled.sem, scaled.prev(w))
                for j in range(SUB):
                    dve.wait_ge(stat.sem, stat.now(w, 2 * j + 1))
                    hop(dve, passed)
                    dve.bn_aggr(mv[:, j, :], stats[:, j, :]).then_inc(aggr.sem, 1)
                dve.wait_ge(rooted.sem, rooted.now(w))
                dve.wait_ge(xn_ready.sem, xn_ready.prev(w))
                dve.reciprocal(rstd[:], sd[:]).then_inc(scaled.sem, 1)
                dve.wait_ge(scaled.sem, scaled.now(w, 0))
                dve.scalar_tensor_tensor(nmr[:], mv[:, :, 0], -1.0, rstd[:], ALU.mult,
                                         ALU.mult).then_inc(scaled.sem, 1)

            def shifted(w):
                for b in range(CB):
                    dve.wait_ge(h_ready.sem, h_ready.now(w, b))
                    if b >= 2:
                        dve.wait_ge(xxx_ready.sem, xxx_ready.now(w, b - 2))
                    else:
                        dve.wait_ge(xxx_ready.sem, xxx_ready.prev(w, CB - 2 + b))
                    dve.wait_ge(carried.sem, carried.prev(w, b))
                    dve.tensor_tensor(xx[:, b % 2, :], h[:, b, 0:WIN], h[:, b, 1:WIN + 1],
                                      ALU.subtract).then_inc(xx_ready.sem, 1)
                    dve.wait_ge(xx_ready.sem, xx_ready.now(w, b))
                    if b >= 4:
                        dve.wait_ge(z_step.sem, z_step.now(w, b - 4))
                    else:
                        dve.wait_ge(z_step.sem, z_step.prev(w, CB - 4 + b))
                    dve.scalar_tensor_tensor(xxx[:, b % 4, :], xx[:, b % 2, :], maa[:, b:b + 1],
                                             h[:, b, 1:WIN + 1], ALU.mult,
                                             ALU.add).then_inc(xxx_ready.sem, 1)

            def z_low(w):
                for n, (low, full, high) in enumerate(((za_lo, za, za_hi), (zb_lo, zb, zb_hi))):
                    dve.wait_ge(z_hi.sem, z_hi.now(w, n))
                    dve.wait_ge(z_stored.sem, z_stored.prev(w))
                    dve.tensor_tensor(low[:], full[:], high[:].bitcast(F32),
                                      ALU.subtract).then_inc(z_lo.sem, 1)

            statistics(0, 0, 0)

            def body(w, pair, parity):
                if not isinstance(w, int) or w + 1 < NW:
                    statistics(w + 1, pair + parity, 1 - parity)
                if not isinstance(w, int) or w:
                    z_low(w - 1)
                shifted(w)

            windows(dve, body)
            z_low(NW - 1)

        @block.scalar
        def _(act):
            for s in (rooted, xn_ready, h_ready, z_tanh, z_hi, z_stored, *h_stored):
                s.grant(act)
            act.wait_ge(zeroed, 3)

            def root(w):
                act.wait_ge(aggr.sem, aggr.now(w))
                act.wait_ge(scaled.sem, scaled.prev(w))
                act.activation(sd[:], mv[:, :, 1], ACT.Sqrt, bias=eps[:]).then_inc(rooted.sem, 1)

            def normalise(w, q):
                act.wait_ge(scaled.sem, scaled.now(w))
                act.wait_ge(turned.sem, turned.prev(w))
                for j in range(SUB):
                    act.activation(xn[:, j, :], xb[:, q, j, :], ACT.Identity, bias=nmr[:, j:j + 1],
                                   scale=rstd[:, j:j + 1]).then_inc(xn_ready.sem, 1)

            def copy_h(w):
                for b in range(CB):
                    act.wait_ge(turned.sem, turned.now(w, b))
                    act.wait_ge(carried.sem, carried.prev(w, b))
                    act.wait_ge(xxx_ready.sem, xxx_ready.prev(w, b))
                    act.wait_ge(h_stored[b].sem, h_stored[b].prev(w))
                    act.copy(h[:, b, 1:WIN + 1], ps_t[b % 4][:]).then_inc(h_ready.sem, 1)
                    act.wait_ge(h_ready.sem, h_ready.now(w, b))
                    act.dma_start(hT[:, b, bass.ds(w * WIN + 1, WIN)],
                                  h[:, b, 1:WIN + 1]).then_inc(h_stored[b].sem, 16)

            def finish_z(w):
                act.wait_ge(z_step.sem, z_step.now(w))
                act.wait_ge(z_lo.sem, z_lo.prev(w))
                act.activation(za[:], ps_za[:], ACT.Tanh).then_inc(z_tanh.sem, 1)
                act.activation(zb[:], ps_zb[:], ACT.Tanh).then_inc(z_tanh.sem, 1)
                act.wait_ge(z_stored.sem, z_stored.prev(w))
                for n, (hi, full) in enumerate(((za_hi, za), (zb_hi, zb))):
                    act.wait_ge(z_tanh.sem, z_tanh.now(w, n))
                    act.copy(hi[:], full[:]).then_inc(z_hi.sem, 1)

            def store_z(w):
                act.wait_ge(z_lo.sem, z_lo.now(w))
                act.wait_ge(z_hi.sem, z_hi.now(w))
                cols = bass.ds(w * WIN, WIN)
                for part, (a, bb) in enumerate(((za_hi, zb_hi), (za_lo, zb_lo), (za_hi, zb_hi))):
                    rows = slice(part * DMIX, part * DMIX + DMIX)
                    act.dma_start(zs[0:4, rows, cols], a[:].bitcast(F32)).then_inc(z_stored.sem, 16)
                    act.dma_start(zs[4, rows, cols], bb[:].bitcast(F32)).then_inc(z_stored.sem, 16)

            root(0)
            normalise(0, 0)

            def body(w, pair, parity):
                more = not isinstance(w, int) or w + 1 < NW
                if more:
                    root(w + 1)
                copy_h(w)
                if not isinstance(w, int) or w:
                    store_z(w - 1)
                if more:
                    normalise(w + 1, 1 - parity)
                finish_z(w)

            windows(act, body)
            store_z(NW - 1)
            act.wait_ge(z_stored.sem, z_stored.now(NW - 1))
            act.wait_ge(zero_stored, 16)
            for s in h_stored:
                act.wait_ge(s.sem, s.now(NW - 1))

        @block.tensor
        def _(pe):
            for s in (turned, z_step):
                s.grant(pe)
            pe.wait_ge(consts, 48)
            with pe.Fori(0, NW) as w:
                pe.wait_ge(xn_ready.sem, xn_ready.now(w))
                for b in range(CB):
                    if b >= 4:
                        pe.wait_ge(h_ready.sem, h_ready.now(w, b - 4))
                    else:
                        pe.wait_ge(h_ready.sem, h_ready.prev(w, CB - 4 + b))
                    for j in range(SUB):
                        mm = pe.transpose(ps_t[b % 4][:, j * P:(j + 1) * P],
                                          xn[:, j, b * P:(b + 1) * P], ident[:])
                    mm.then_inc(turned.sem, 1)
                pe.wait_ge(z_tanh.sem, z_tanh.prev(w))
                for b in range(CB):
                    pe.wait_ge(xxx_ready.sem, xxx_ready.now(w, b))
                    pe.matmul(ps_za[:], w1s[:, b, 0:P], xxx[:, b % 4, :], start=b == 0, stop=b == CB - 1)
                    pe.matmul(ps_zb[:], w1s[:, b, P:], xxx[:, b % 4, :], start=b == 0,
                              stop=b == CB - 1).then_inc(z_step.sem, 1)


def load_split(nc, ctx, phase, groups):
    pieces = [(dram[:, b, :], hi[:, b, :], lo[:, b, :]) for dram, hi, lo in groups for b in range(dram.shape[1])]
    SLOTS = 4
    slot = ctx.enter_context(nc.sbuf_tensor(phase.prefix + "wslot", [P, SLOTS, pieces[0][0].shape[1]], F32))
    loaded = [phase.semaphore(f"wloaded{n}") for n in range(SLOTS)]
    high, low = phase.semaphore("whigh"), phase.semaphore("wlow")

    def load(sp, some):
        for n in some:
            if n >= SLOTS:
                sp.wait_ge(low, n - SLOTS + 1)
            sp.dma_start(slot[:, n % SLOTS], pieces[n][0]).then_inc(loaded[n % SLOTS], 16)

    def take_high(act, some):
        for n in some:
            act.wait_ge(loaded[n % SLOTS], 16 * (n // SLOTS + 1))
            act.copy(pieces[n][1], slot[:, n % SLOTS]).then_inc(high, 1)

    def take_low(dve, some):
        for n in some:
            _, hi, lo = pieces[n]
            dve.wait_ge(high, n + 1)
            dve.tensor_tensor(lo, slot[:, n % SLOTS], hi.bitcast(F32), ALU.subtract).then_inc(low, 1)

    return load, take_high, take_low, low


def streams_phase(nc, hT, zs, w2_dram, streams, factors, factors_sum):
    with ExitStack() as ctx:
        sb = lambda name, shape, dt=F32: ctx.enter_context(nc.sbuf_tensor("p_" + name, shape, dt))
        phase = ctx.enter_context(Phase(nc, "p_"))
        sig, sem = phase.counter, phase.semaphore
        NS = len(streams)
        TOTAL = NS * NW
        maas = sb("maa", [P, NS, CB])
        w2 = sb("w2", [3 * DMIX, 2, C], F32R)
        w2_full = sb("w2full", [3 * DMIX, C])
        z = sb("z", [3 * DMIX, 2, WIN], F32R)
        h = sb("h", [P, CB, WIN + 1])
        xx, prod, xf = (sb(n, [P, 2, WIN]) for n in ("xx", "prod", "xf"))
        stage = sb("stage", [P, 4, WIN])
        hi, lo = sb("hi", [P, 2, CB, WIN], F32R), sb("lo", [P, 2, CB, WIN], F32R)
        w_slot = sb("wslot", [P, 2, CB, P])
        w_hi, w_lo = sb("whi", [P, CB, C], F32R), sb("wlo", [P, CB, C], F32R)
        factor = sb("factor", [P, 4, WIN])
        fsum = sb("fsum", [P, WIN])
        factor_rows = factors.rearrange("r a (h n) -> r (a h) n", n=WIN)
        sum_rows = factors_sum.rearrange("a (h n) -> (a h) n", n=WIN)
        assert sum_rows.shape[0] == TOTAL // 2 * P
        ps_mix = [ctx.enter_context(nc.psum_tensor(f"p_mix{b}", [P, WIN], F32)) for b in range(2)]
        ps_out = [ctx.enter_context(nc.psum_tensor(f"p_out{b}", [P, WIN], F32)) for b in range(4)]

        consts, w2_loaded, w2_ready = sem("consts"), sem("w2_loaded"), sem("w2_ready")
        z_loaded = [sem(f"z_loaded{n}") for n in range(2)]
        h_loaded = [sem(f"h_loaded{b}") for b in range(CB)]
        w_loaded = [sem(f"w_loaded{n}") for n in range(2)]
        w_high, w_low, passed = sem("w_high"), sem("w_low"), sem("passed")
        stored = [sig(f"stored{n}", 2 * 16) for n in range(4)]
        factor_loaded = [sem(f"factor_loaded{n}") for n in range(4)]
        sum_stored = sig("sum_stored", 16)
        added = sig("added", RANK - 1)
        mixed = sig("mixed", CB)
        xx_ready = sig("xx_ready", CB)
        prod_ready = sig("prod_ready", CB)
        xf_ready = sig("xf_ready", CB)
        hi_ready = sig("hi_ready", CB)
        lo_ready = sig("lo_ready", CB)
        out_done = sig("out_done", CB)
        copied = sig("copied", CB)
        block = ctx.enter_context(nc.Block())

        def wait_back(eng, counter, w, k, n):
            eng.wait_ge(counter.sem, counter.prev(w, (k - n) % CB) if k < n else counter.now(w, k - n))

        def windows(eng, body):
            for s in range(NS):
                first = s * NW // 2
                with eng.Fori(0, NW // 2 - 1) as pair:
                    for parity in range(2):
                        local = 2 * pair + parity
                        body(local + s * NW, local, pair + first, parity, s, None)
                pair = NW // 2 - 1
                for parity in range(2):
                    local = 2 * pair + parity
                    body(local + s * NW, local, pair + first, parity, s, 1 - parity)

        def columns_of(n):
            return slice(n * P, n * P + P)

        @block.sync
        def _(sp):
            for s in (*stored, sum_stored):
                s.grant(sp)
            with nc.allow_non_contiguous_dma(reason="vectors of channels"):
                for n, (_, _, maa, _, _) in enumerate(streams):
                    sp.dma_start(maas[:, n, :], columns(maa)).then_inc(consts, 16)

            def load_w2(s):
                if s:
                    sp.wait_ge(w2_ready, 2 * s)
                for part in range(3):
                    sp.dma_start(w2_full[part * DMIX:(part + 1) * DMIX, :],
                                 w2_dram[streams[s][1]]).then_inc(w2_loaded, 16)

            def load_z(s, local, parity):
                sp.dma_start(z[:, parity].bitcast(F32),
                             zs[streams[s][1], :, bass.ds(local * WIN, WIN)]).then_inc(z_loaded[parity], 16)

            def load_h(local, b):
                sp.dma_start(h[:, b, :], hT[:, b, bass.ds(local * WIN, WIN + 1)]).then_inc(h_loaded[b], 16)

            def load_piece(s, n):
                m = CB * s + n
                if m >= 2:
                    sp.wait_ge(w_low, m - 1)
                sp.dma_start(w_slot[:, n % 2], streams[s][3][:, :, columns_of(n)]).then_inc(w_loaded[n % 2], 16)

            def load_factor(pair, r):
                if r >= 4:
                    sp.wait_ge(added.sem, added.now(pair, max(r - 5, 0)))
                elif not isinstance(pair, int) or pair:
                    sp.wait_ge(added.sem, added.prev(pair, r + 3))
                sp.dma_start(factor[:, r % 4], factor_rows[r, bass.ds(pair * P, P), :]
                             ).then_inc(factor_loaded[r % 4], 16)

            load_w2(0)
            load_z(0, 0, 0)
            for b in range(CB):
                load_h(0, b)
            load_z(0, 1, 1)
            for n in range(4):
                load_factor(0, n)
            for n in range(CB):
                load_piece(0, n)
            for b in range(CB):
                sp.wait_ge(xf_ready.sem, xf_ready.now(0, b))
                load_h(1, b)
            load_w2(1)
            for n in range(4, RANK):
                load_factor(0, n)

            def body(w, local, pair, parity, s, left):
                more = left is None or s + 1 < NS
                after = (s, local + 2) if left is None else (s + 1, 1 - left)
                if more:
                    sp.wait_ge(mixed.sem, mixed.now(w))
                    hop(sp, passed)
                    load_z(*after, parity)
                if parity:
                    sp.wait_ge(added.sem, added.now(pair))
                    sp.dma_start(sum_rows[bass.ds(pair * P, P), :], fsum[:]).then_inc(sum_stored.sem, 16)
                for b in range(CB):
                    if more and b % 2:
                        load_factor(pair + 1, 4 * parity + b // 2)
                    if more:
                        sp.wait_ge(xf_ready.sem, xf_ready.now(w + 1, b))
                        if b == 0:
                            hop(sp, passed)
                        load_h(after[1], b)
                    if left == 0 and s + 1 < NS:
                        load_piece(s + 1, b)
                    kind, out = streams[s][0], streams[s][4]
                    sp.wait_ge(copied.sem, copied.now(w, b))
                    if kind == "v":
                        dst = out[bass.ds(local * WIN + (b // 2) * P, P), (b % 2) * WIN:(b % 2 + 1) * WIN]
                    else:
                        dst = out[:, b, bass.ds(local * WIN, WIN)]
                    sp.dma_start(dst, stage[:, b % 4, :]).then_inc(stored[b % 4].sem, 16)
                if left == 0 and s + 2 < NS:
                    load_w2(s + 2)

            windows(sp, body)
            sp.wait_ge(sum_stored.sem, sum_stored.now(TOTAL // 2 - 1))
            for s in stored:
                sp.wait_ge(s.sem, s.now(TOTAL - 1))

        @block.gpsimd
        def _(pool):
            for s in (xx_ready, added):
                s.grant(pool)

            def add_factor(pair, r):
                pool.wait_ge(factor_loaded[r % 4], 16 * (2 * pair + r // 4 + 1))
                if r == 0:
                    return
                if r == 1:
                    pool.wait_ge(sum_stored.sem, sum_stored.prev(pair))
                    pool.tensor_tensor(fsum[:], factor[:, 0], factor[:, 1], ALU.add).then_inc(added.sem, 1)
                else:
                    pool.wait_ge(added.sem, added.now(pair, r - 2))
                    pool.tensor_tensor(fsum[:], fsum[:], factor[:, r % 4], ALU.add).then_inc(added.sem, 1)

            with pool.Fori(0, TOTAL // 2) as pair:
                for parity in range(2):
                    w = 2 * pair + parity
                    for b in range(CB):
                        pool.wait_ge(h_loaded[b], 16 * (w + 1))
                        wait_back(pool, prod_ready, w, b, 2)
                        pool.tensor_tensor(xx[:, b % 2, :], h[:, b, 0:WIN], h[:, b, 1:WIN + 1],
                                           ALU.subtract).then_inc(xx_ready.sem, 1)
                        if b % 2:
                            add_factor(pair, 4 * parity + b // 2)

        @block.vector
        def _(dve):
            for s in (prod_ready, xf_ready, lo_ready):
                s.grant(dve)
            dve.wait_ge(consts, 16 * NS)

            def split_w2(s):
                dve.wait_ge(w2_loaded, 48 * (s + 1))
                if s >= 2:
                    dve.wait_ge(mixed.sem, mixed.now((s - 1) * NW - 1))
                mine = w2[:, s % 2, :]
                dve.tensor_copy(mine, w2_full[:]).then_inc(w2_ready, 1)
                dve.wait_ge(w2_ready, 2 * s + 1)
                third = w2[2 * DMIX:, s % 2, :]
                dve.tensor_tensor(third, w2_full[2 * DMIX:, :], third.bitcast(F32),
                                  ALU.subtract).then_inc(w2_ready, 1)

            def piece_low(s, n):
                dve.wait_ge(w_high, CB * s + n + 1)
                cols = columns_of(n)
                dve.tensor_tensor(w_lo[:, :, cols], w_slot[:, n % 2], w_hi[:, :, cols].bitcast(F32),
                                  ALU.subtract).then_inc(w_low, 1)

            def low(w, parity, b):
                dve.wait_ge(hi_ready.sem, hi_ready.now(w, b))
                dve.tensor_tensor(lo[:, parity, b, :], xf[:, b % 2, :], hi[:, parity, b, :].bitcast(F32),
                                  ALU.subtract).then_inc(lo_ready.sem, 1)

            def mix(w, s, b):
                dve.wait_ge(xx_ready.sem, xx_ready.now(w, b))
                dve.wait_ge(mixed.sem, mixed.now(w, b))
                wait_back(dve, xf_ready, w, b, 2)
                dve.scalar_tensor_tensor(prod[:, b % 2, :], ps_mix[b % 2][:], maas[:, s, b:b + 1],
                                         xx[:, b % 2, :], ALU.add, ALU.mult).then_inc(prod_ready.sem, 1)
                dve.wait_ge(prod_ready.sem, prod_ready.now(w, b))
                wait_back(dve, lo_ready, w, b, 2)
                dve.tensor_tensor(xf[:, b % 2, :], prod[:, b % 2, :], h[:, b, 1:WIN + 1],
                                  ALU.add).then_inc(xf_ready.sem, 1)

            def window(w, parity, s, pieces=False):
                for b in range(CB):
                    mix(w, s, b)
                    if b >= 1:
                        low(w, parity, b - 1)
                        if pieces:
                            piece_low(s, b - 1)
                low(w, parity, CB - 1)
                if pieces:
                    piece_low(s, CB - 1)

            split_w2(0)
            window(0, 0, 0)
            for n in range(CB):
                piece_low(0, n)

            def body(w, local, pair, parity, s, left):
                if left == 1 and s + 1 < NS:
                    split_w2(s + 1)
                after = s + 1 if left == 0 else s
                if after < NS:
                    dve.wait_ge(out_done.sem, out_done.prev(w))
                    window(w + 1, 1 - parity, after, pieces=left == 0)

            windows(dve, body)

        @block.scalar
        def _(act):
            for s in (hi_ready, copied):
                s.grant(act)

            def piece_high(s, n):
                act.wait_ge(w_loaded[n % 2], 16 * (CB // 2 * s + n // 2 + 1))
                if s:
                    act.wait_ge(out_done.sem, out_done.now(s * NW - 1, n))
                act.copy(w_hi[:, :, columns_of(n)], w_slot[:, n % 2]).then_inc(w_high, 1)

            def high(w, parity, b):
                act.wait_ge(xf_ready.sem, xf_ready.now(w, b))
                act.copy(hi[:, parity, b, :], xf[:, b % 2, :]).then_inc(hi_ready.sem, 1)

            def evacuate(w, s, b):
                act.wait_ge(out_done.sem, out_done.now(w, b))
                act.wait_ge(stored[b % 4].sem, stored[b % 4].prev(w) if b < 4
                            else stored[b % 4].now(w, 15))
                function = ACT.Silu if streams[s][0] == "g" else ACT.Copy
                act.activation(stage[:, b % 4, :], ps_out[b % 4][:], function).then_inc(copied.sem, 1)

            for b in range(CB):
                high(0, 0, b)
            for n in range(CB):
                piece_high(0, n)

            def body(w, local, pair, parity, s, left):
                act.wait_ge(out_done.sem, out_done.prev(w))
                for b in range(CB):
                    if left != 0 or s + 1 < NS:
                        high(w + 1, 1 - parity, b)
                    evacuate(w, s, b)
                    if left == 0 and s + 1 < NS:
                        piece_high(s + 1, b)

            windows(act, body)

        @block.tensor
        def _(pe):
            for s in (mixed, out_done):
                s.grant(pe)

            def mix(w, pair, parity, s, b):
                if b == 0:
                    pe.wait_ge(w2_ready, 2 * (s + 1))
                    pe.wait_ge(z_loaded[parity], 16 * (pair + 1))
                wait_back(pe, prod_ready, w, b, 2)
                pe.matmul(ps_mix[b % 2][:], w2[:, s % 2, b * P:(b + 1) * P], z[:, parity],
                          start=True, stop=True).then_inc(mixed.sem, 1)

            def output(w, parity, s, n):
                wait_back(pe, copied, w, n, 4)
                by_tokens = streams[s][0] == "v"
                pe.wait_ge(w_low, CB * s + (min(CB // 2 * (n + 1), CB) if by_tokens else n + 1))
                for b in range(CB):
                    if n == 0:
                        pe.wait_ge(lo_ready.sem, lo_ready.now(w, b))
                    for xs, ws in ((hi, w_hi), (hi, w_lo), (lo, w_hi)):
                        if by_tokens:
                            left = xs[:, parity, b, (n // 2) * P:(n // 2 + 1) * P]
                            right = ws[:, b, (n % 2) * WIN:(n % 2 + 1) * WIN]
                        else:
                            left, right = ws[:, b, n * P:(n + 1) * P], xs[:, parity, b, :]
                        mm = pe.matmul(ps_out[n % 4][:], left, right, start=b == 0 and xs is hi and ws is w_hi,
                                       stop=b == CB - 1 and xs is lo)
                mm.then_inc(out_done.sem, 1)

            for b in range(CB):
                mix(0, 0, 0, 0, b)

            def body(w, local, pair, parity, s, left):
                after = s + 1 if left == 0 else s
                for b in range(CB):
                    if after < NS:
                        mix(w + 1, pair + parity, 1 - parity, after, b)
                    output(w, parity, s, b)

            windows(pe, body)


def decay_phase(nc, hT, zs, w2_dram, maa, dw1_dram, dw2_dram, bias_dram, out):
    with ExitStack() as ctx:
        sb = lambda name, shape, dt=F32: ctx.enter_context(nc.sbuf_tensor("d_" + name, shape, dt))
        phase = ctx.enter_context(Phase(nc, "d_"))
        sig, sem = phase.counter, phase.semaphore
        maas = sb("maa", [P, CB])
        w2 = sb("w2", [3 * DMIX, C], F32R)
        w2_full = sb("w2full", [3 * DMIX, C])
        z = sb("z", [3 * DMIX, T], F32R)
        h = sb("h", [P, CB, WIN + 1])
        xx = sb("xx", [P, 2, WIN])
        prod = sb("prod", [P, 2, WIN])
        stage = sb("stage", [P, 4, WIN])
        xf = sb("xf", [P, 2 * CB, WIN])
        dw1 = sb("dw1", [P, CB, DDEC])
        dw2 = sb("dw2", [DDEC, C])
        bias = sb("bias", [P, CB])
        td = sb("td", [DDEC, WIN])
        rate = sb("rate", [P, 2, WIN])
        ps_mix = [ctx.enter_context(nc.psum_tensor(f"d_mix{b}", [P, WIN], F32)) for b in range(2)]
        ps_out = [ctx.enter_context(nc.psum_tensor(f"d_out{b}", [P, WIN], F32)) for b in range(4)]
        ps_d = ctx.enter_context(nc.psum_tensor("d_psd", [DDEC, WIN], F32))

        consts, z_loaded = sem("consts"), sem("z_loaded")
        h_loaded = [sem(f"h_loaded{b}") for b in range(CB)]
        stored = [sig(f"stored{n}", 2 * 16) for n in range(4)]
        w2_ready = sem("w2_ready")
        mixed = sig("mixed", CB)
        xx_ready = sig("xx_ready", CB)
        prod_ready = sig("prod_ready", CB)
        xf_ready = sig("xf_ready", CB)
        out_done = sig("out_done", CB)
        copied = sig("copied", CB)
        d_done = sig("d_done")
        td_ready = sig("td_ready")
        rated = sig("rated", CB)
        block = ctx.enter_context(nc.Block())
        n_consts = 16 * 8

        def back(n, k):
            return (k - n) % CB, k < n

        def wait_back(eng, signal, w, k, n):
            j, before = back(n, k)
            eng.wait_ge(signal.sem, signal.prev(w, j) if before else signal.now(w, j))

        def windows(eng, body):
            with eng.Fori(0, NW // 2 - 1) as pair:
                for parity in range(2):
                    body(2 * pair + parity, parity, False)
            body(NW - 2, 0, False)
            body(NW - 1, 1, True)

        @block.sync
        def _(sp):
            for s in stored:
                s.grant(sp)
            with nc.allow_non_contiguous_dma(reason="one vector of channels"):
                sp.dma_start(maas[:], columns(maa)).then_inc(consts, 16)
                sp.dma_start(bias[:], columns(bias_dram)).then_inc(consts, 16)
            for part in range(3):
                sp.dma_start(w2_full[part * DMIX:(part + 1) * DMIX, :], w2_dram).then_inc(consts, 16)
            sp.dma_start(z[:].bitcast(F32), zs).then_inc(consts, 16)
            sp.dma_start(dw1[:], dw1_dram.rearrange("(b p) d -> p b d", p=P)).then_inc(consts, 16)
            sp.dma_start(dw2[:], dw2_dram).then_inc(consts, 16)

            def load_h(w, b):
                sp.dma_start(h[:, b, :], hT[:, b, bass.ds(w * WIN, WIN + 1)]).then_inc(h_loaded[b], 16)

            for b in range(CB):
                load_h(0, b)
            for b in range(CB):
                sp.wait_ge(xf_ready.sem, xf_ready.now(0, b))
                load_h(1, b)

            def body(w, parity, last):
                for b in range(CB):
                    if not last and not (isinstance(w, int) and w + 2 >= NW):
                        sp.wait_ge(xf_ready.sem, xf_ready.now(w + 1, b))
                        load_h(w + 2, b)
                    sp.wait_ge(copied.sem, copied.now(w, b))
                    sp.dma_start(out[:, b, bass.ds(w * WIN, WIN)], stage[:, b % 4, :]).then_inc(stored[b % 4].sem, 16)

            windows(sp, body)
            for s in stored:
                sp.wait_ge(s.sem, s.now(NW - 1))

        @block.gpsimd
        def _(pool):
            xx_ready.grant(pool)

            def shift(w, b):
                pool.wait_ge(h_loaded[b], 16 * (w + 1))
                wait_back(pool, prod_ready, w, b, 2)
                pool.tensor_tensor(xx[:, b % 2, :], h[:, b, 0:WIN], h[:, b, 1:WIN + 1],
                                   ALU.subtract).then_inc(xx_ready.sem, 1)

            with pool.Fori(0, NW) as w:
                for b in range(CB):
                    shift(w, b)

        @block.vector
        def _(dve):
            for s in (prod_ready, xf_ready):
                s.grant(dve)
            dve.wait_ge(consts, n_consts)
            dve.tensor_copy(w2[:], w2_full[:]).then_inc(w2_ready, 1)
            dve.wait_ge(w2_ready, 1)
            dve.tensor_tensor(w2[2 * DMIX:, :], w2_full[2 * DMIX:, :], w2[2 * DMIX:, :].bitcast(F32),
                              ALU.subtract).then_inc(w2_ready, 1)

            def mix(w, parity, b):
                dve.wait_ge(xx_ready.sem, xx_ready.now(w, b))
                dve.wait_ge(mixed.sem, mixed.now(w, b))
                wait_back(dve, xf_ready, w, b, 2)
                dve.scalar_tensor_tensor(prod[:, b % 2, :], ps_mix[b % 2][:], maas[:, b:b + 1],
                                         xx[:, b % 2, :], ALU.add, ALU.mult).then_inc(prod_ready.sem, 1)
                dve.wait_ge(prod_ready.sem, prod_ready.now(w, b))
                if not isinstance(w, int) or w >= 2:
                    dve.wait_ge(d_done.sem, d_done.prev(w) - 1)
                dve.tensor_tensor(xf[:, parity * CB + b, :], prod[:, b % 2, :], h[:, b, 1:WIN + 1],
                                  ALU.add).then_inc(xf_ready.sem, 1)

            def window(w, parity):
                for b in range(CB):
                    mix(w, parity, b)

            window(0, 0)

            def body(w, parity, last):
                if not last:
                    window(w + 1, 1 - parity)

            windows(dve, body)

        @block.scalar
        def _(act):
            for s in (copied, td_ready, rated):
                s.grant(act)
            act.wait_ge(consts, n_consts)

            def evacuate(w, b):
                act.wait_ge(out_done.sem, out_done.now(w, b))
                wait_back(act, copied, w, b, 2)
                act.activation(rate[:, b % 2, :], ps_out[b % 4][:], ACT.Exp,
                               bias=bias[:, b:b + 1]).then_inc(rated.sem, 1)
                act.wait_ge(rated.sem, rated.now(w, b))
                act.wait_ge(stored[b % 4].sem, stored[b % 4].prev(w) if b < 4
                            else stored[b % 4].now(w, 15))
                act.activation(stage[:, b % 4, :], rate[:, b % 2, :], ACT.Exp, scale=-1.0).then_inc(copied.sem, 1)

            def body(w, parity, last):
                act.wait_ge(d_done.sem, d_done.now(w))
                act.wait_ge(out_done.sem, out_done.prev(w))
                act.activation(td[:], ps_d[:], ACT.Tanh).then_inc(td_ready.sem, 1)
                for b in range(CB):
                    evacuate(w, b)

            windows(act, body)

        @block.tensor
        def _(pe):
            for s in (mixed, out_done, d_done):
                s.grant(pe)
            pe.wait_ge(consts, n_consts)
            pe.wait_ge(w2_ready, 2)

            def mix(w, b):
                wait_back(pe, prod_ready, w, b, 2)
                pe.matmul(ps_mix[b % 2][:], w2[:, b * P:(b + 1) * P], z[:, bass.ds(w * WIN, WIN)],
                          start=True, stop=True).then_inc(mixed.sem, 1)

            for b in range(CB):
                mix(0, b)

            def body(w, parity, last):
                for b in range(CB):
                    pe.wait_ge(xf_ready.sem, xf_ready.now(w, b))
                    mm = pe.matmul(ps_d[:], dw1[:, b, :], xf[:, parity * CB + b, :],
                                   start=b == 0, stop=b == CB - 1)
                mm.then_inc(d_done.sem, 1)
                for n in range(CB):
                    if not last:
                        mix(w + 1, n)
                    if n == 0:
                        pe.wait_ge(td_ready.sem, td_ready.now(w))
                    wait_back(pe, copied, w, n, 4)
                    pe.matmul(ps_out[n % 4][:], dw2[:, n * P:(n + 1) * P], td[:], start=True,
                              stop=True).then_inc(out_done.sem, 1)

            windows(pe, body)


def recurrence_phase(nc, rT, kT, wT, gT, v, faaaa, gamma, beta, ident_dram, mask_dram, yT):
    with ExitStack() as ctx:
        sb = lambda name, shape, dt=F32: ctx.enter_context(nc.sbuf_tensor("r_" + name, shape, dt))
        ps = lambda name, shape: ctx.enter_context(nc.psum_tensor("r_" + name, shape, F32))
        phase = ctx.enter_context(Phase(nc, "r_"))
        sig, sem = phase.counter, phase.semaphore
        HALF = CHUNK // 2
        GB = CB // 2

        ident = sb("ident", [P, P])
        masks = sb("masks", [P, LEVELS, HALF], I32)
        bonus = sb("bonus", [P, CB, 2])
        gam, bet = sb("gam", [P, CB]), sb("bet", [P, CB])
        rb, kb, wb, gb = (sb(n, [P, 2, CB, CHUNK]) for n in ("rb", "kb", "wb", "gb"))
        vb = sb("vb", [P, 2, C])
        rbd = sb("rbd", [P, 2, CB, 2 * HALF])
        decays = sb("decays", [P, 2, CB * CHUNK])
        at = sb("at", [P, 2, H, CHUNK])
        rk = sb("rk", [P, CB, CHUNK])
        dsb = sb("dsb", [P, H])
        dv = sb("dv", [P, C])
        kt = sb("kt", [P, C])
        state = sb("state", [P, 2, CB, P])
        ob, cen, sq, nrm = (sb(n, [P, C]) for n in ("ob", "cen", "sq", "nrm"))
        gsum, gmean, gvar, gve, gsd, grs = (sb(n, [P, H]) for n in ("gsum", "gmean", "gvar", "gve", "gsd", "grs"))
        yt, yb = sb("yt", [P, CB, CHUNK]), sb("yb", [P, CB, CHUNK])
        ps_a = [[ps(f"a{s}{g}", [P, 512]) for g in range(2)] for s in range(2)]
        ps_o = [ps(f"o{n}", [P, 512]) for n in range(2)]
        ps_s, ps_d = ps("s", [P, 512]), ps("d", [P, H])

        consts, zeroed = sem("consts"), sem("zeroed")
        kw_loaded = [sem(f"kw_loaded{n}") for n in range(2)]
        rv_loaded = [sem(f"rv_loaded{n}") for n in range(2)]
        g_loaded = [sem(f"g_loaded{n}") for n in range(2)]
        y_stored = sig("y_stored", 16)
        passed = sem("passed")
        d_done = sig("d_done")
        a_done = sig("a_done", 2 * LEVELS)
        nt_done = sig("nt_done", 2)
        kt_done = sig("kt_done", 2)
        s_done = sig("s_done", 2)
        o_done = sig("o_done", 2)
        p_done = sig("p_done", LEVELS)
        cp_done = sig("cp_done", 2 * 5)
        r_done = sig("r_done", 2 * LEVELS)
        o_read = sig("o_read", 2)
        gn = sig("gn", 6)
        s_added = sig("s_added", 4)
        y_done = sig("y_done")
        d_copied = sig("d_copied")
        rbd_done = sig("rbd_done", 4 * LEVELS)
        sq_done = sig("sq_done")
        wide_done = sig("wide_done", 4)
        rooted = sig("rooted")
        yt_done = sig("yt_done", CB)
        kt_copied = sig("kt_copied", 2)
        rk_done = sig("rk_done")
        k_done = sig("k_done", 2 * LEVELS)
        dv_done = sig("dv_done")
        s_mult = sig("s_mult")
        n_done = sig("n_done")
        block = ctx.enter_context(nc.Block())

        def decay_view(parity, level):
            if level == 0:
                return wb[:, parity]
            at_col = CB * sum(CHUNK >> m for m in range(1, level))
            n = CHUNK >> level
            return decays[:, parity, at_col:at_col + CB * n].rearrange("p (b n) -> p b n", n=n)

        def halves(ap, level):
            return ap.rearrange("p b (j u q) -> p b j u q", u=2, q=1 << level)

        def by(ap, shape):
            return ap.unsqueeze(len(ap.shape)).to_broadcast(shape)

        def steps(eng, body):
            for i in range(4):
                body(i, i // 2, i % 2)
            with eng.Fori(2, NCH // 2 - 1) as pair:
                for parity in range(2):
                    body(2 * pair + parity, pair, parity)
            for i in range(NCH - 2, NCH + 3):
                body(i, i // 2, i % 2)

        def has(i, back=0):
            return not isinstance(i, int) or 0 <= i - back < NCH

        def old(counter, i, back, k=None):
            if isinstance(i, int) and i - back < 0:
                return counter.now(-1)
            return counter.now(i - back, k)

        def use_of(pair, parity, of):
            return pair + (parity + of) // 2

        heads = lambda ap: ap.rearrange("p (h m) -> p h m", m=HEAD)
        head_cols = [P, H, HEAD]

        KT = LEVELS
        bank_pair = lambda n: ps_a[n % 2]

        MASKED = 5
        UNMASKED = {5: [(0, 32), (64, 96)], 6: [(0, 64)]}

        def wait_bank(eng, n, i, g):
            if n == 1:
                eng.wait_ge(kt_copied.sem, kt_copied.now(i - 1, g))
            elif n == 0:
                eng.wait_ge(wide_done.sem, wide_done.now(i - 1, 2 * (LEVELS - 1 - MASKED) + g))
            elif n - 2 < MASKED:
                eng.wait_ge(cp_done.sem, cp_done.now(i, 2 * (n - 2) + g))
            else:
                eng.wait_ge(wide_done.sem, wide_done.now(i, 2 * (n - 2 - MASKED) + g))

        @block.sync
        def _(sp):
            y_stored.grant(sp)
            sp.dma_start(ident[:], ident_dram).then_inc(consts, 16)
            sp.dma_start(masks[:], mask_dram).then_inc(consts, 16)
            sp.wait_ge(zeroed, 5)
            with nc.allow_non_contiguous_dma(reason="vectors of channels"):
                sp.dma_start(gam[:], columns(gamma)).then_inc(consts, 16)
                sp.dma_start(bet[:], columns(beta)).then_inc(consts, 16)
                u = faaaa.rearrange("(b j) n -> j n b", j=2)
                for j in range(2):
                    sp.dma_start(bonus[HEAD * j:HEAD * (j + 1), :, j], u[j]).then_inc(consts, 16)

            def load_kw(i, parity, of):
                q = (parity + of) % 2
                cols = bass.ds((i + of) * CHUNK, CHUNK)
                for tile, src in ((wb, wT), (kb, kT)):
                    sp.dma_start(tile[:, q], src[:, :, cols]).then_inc(kw_loaded[q], 16)

            def load_rv(i, parity, of):
                q = (parity + of) % 2
                cols = bass.ds((i + of) * CHUNK, CHUNK)
                sp.dma_start(rb[:, q], rT[:, :, cols]).then_inc(rv_loaded[q], 16)
                sp.dma_start(vb[:, q], v[cols, :]).then_inc(rv_loaded[q], 16)

            load_kw(0, 0, 0)
            load_rv(0, 0, 0)

            def body(i, pair, parity):
                if has(i, -1):
                    sp.wait_ge(kt_done.sem, kt_done.now(i - 1))
                    sp.wait_ge(r_done.sem, r_done.now(i - 1))
                    load_kw(i, parity, 1)
                if has(i, 1):
                    sp.wait_ge(y_done.sem, old(y_done, i, 3))
                    sp.dma_start(gb[:, 1 - parity], gT[:, :, bass.ds((i - 1) * CHUNK, CHUNK)]
                                 ).then_inc(g_loaded[1 - parity], 16)
                if has(i, 3):
                    sp.wait_ge(y_done.sem, y_done.now(i - 3))
                    sp.dma_start(yT[:, :, bass.ds((i - 3) * CHUNK, CHUNK)], yb[:]).then_inc(y_stored.sem, 16)
                if has(i, -1):
                    sp.wait_ge(o_done.sem, o_done.now(i - 1))
                    sp.wait_ge(dv_done.sem, dv_done.now(i - 1))
                    load_rv(i, parity, 1)

            steps(sp, body)
            sp.wait_ge(y_stored.sem, y_stored.now(NCH - 1))

        @block.gpsimd
        def _(pool):
            for s in (rk_done, k_done, dv_done, s_mult, n_done):
                s.grant(pool)
            pool.memset(at[:], 0.0).then_inc(zeroed, 1)

            def products(i, pair, parity, of):
                q = (parity + of) % 2
                pool.wait_ge(kw_loaded[q], 32 * (use_of(pair, parity, of) + 1))
                pool.wait_ge(rv_loaded[q], 32 * (use_of(pair, parity, of) + 1))
                pool.wait_ge(d_done.sem, d_done.now(i + of - 1))
                pool.tensor_tensor(rk[:], rb[:, q], kb[:, q], ALU.mult).then_inc(rk_done.sem, 1)

            def scale_k(i, parity, l, g):
                pool.wait_ge(a_done.sem, a_done.now(i, 2 * l + g))
                if l == 0:
                    pool.wait_ge(rk_done.sem, rk_done.now(i))
                else:
                    pool.wait_ge(p_done.sem, p_done.now(i, l - 1))
                    pool.wait_ge(k_done.sem, k_done.now(i, 2 * (l - 1) + g))
                blocks = slice(GB * g, GB * g + GB)
                left = halves(kb[:, parity, blocks, :], l)[:, :, :, 0, :]
                right_decay = decay_view(parity, l)[:, blocks, 1::2]
                pool.tensor_tensor(left, left, by(right_decay, left.shape), ALU.mult).then_inc(k_done.sem, 1)

            def carry_state(i, parity):
                pool.wait_ge(s_added.sem, s_added.now(i - 1))
                pool.wait_ge(o_done.sem, o_done.now(i - 1))
                pool.wait_ge(p_done.sem, p_done.now(i))
                pool.tensor_tensor(state[:, 1 - parity], state[:, parity],
                                   decay_view(parity, LEVELS).to_broadcast([P, CB, P]),
                                   ALU.mult).then_inc(s_mult.sem, 1)

            def bonus_outputs(i, parity):
                pool.wait_ge(o_read.sem, old(o_read, i, 2))
                pool.wait_ge(d_copied.sem, d_copied.now(i - 1))
                pool.tensor_tensor(heads(dv[:]), heads(vb[:, 1 - parity]), by(dsb[:], head_cols),
                                   ALU.mult).then_inc(dv_done.sem, 1)

            def normed(i):
                pool.wait_ge(gn.sem, gn.now(i - 2, 5))
                pool.wait_ge(nt_done.sem, old(nt_done, i, 3))
                pool.tensor_tensor(heads(nrm[:]), heads(cen[:]), by(grs[:], head_cols),
                                   ALU.mult).then_inc(n_done.sem, 1)

            products(0, 0, 0, 0)

            def body(i, pair, parity):
                for l in range(LEVELS):
                    for g in range(2 if has(i) else 0):
                        scale_k(i, parity, l, g)
                    if l == 0 and has(i, 1):
                        bonus_outputs(i, parity)
                    if l == 2 and has(i, 2):
                        normed(i)
                    if l == 4 and has(i):
                        carry_state(i, parity)
                if has(i) and has(i, -1):
                    products(i, pair, parity, 1)

            steps(pool, body)

        @block.vector
        def _(dve):
            for s in (p_done, cp_done, r_done, o_read, gn, s_added, y_done):
                s.grant(dve)
            for tile in (rbd, state, bonus):
                dve.memset(tile[:], 0.0).then_inc(zeroed, 1)
            dve.memset(dsb[:], 0.0).then_inc(zeroed, 1)
            dve.wait_ge(consts, 16 * 6)
            dve.wait_ge(zeroed, 5)

            def block_decays(i, pair, parity, of):
                q = (parity + of) % 2
                dve.wait_ge(kw_loaded[q], 32 * (use_of(pair, parity, of) + 1))
                dve.wait_ge(k_done.sem, old(k_done, i, 2 - of))
                dve.wait_ge(s_mult.sem, old(s_mult, i, 2 - of))
                dve.wait_ge(r_done.sem, old(r_done, i, 2 - of))
                for l in range(LEVELS):
                    if l:
                        dve.wait_ge(p_done.sem, p_done.now(i + of, l - 1))
                    src = decay_view(q, l)
                    dve.tensor_tensor(decay_view(q, l + 1), src[:, :, 0::2], src[:, :, 1::2],
                                      ALU.mult).then_inc(p_done.sem, 1)

            def scale_r(i, parity, l, g):
                blocks = slice(GB * g, GB * g + GB)
                dve.wait_ge(rbd_done.sem, rbd_done.now(i, 4 * l + 2 * g + 1))
                if l == 0:
                    dve.wait_ge(rk_done.sem, rk_done.now(i))
                else:
                    dve.wait_ge(p_done.sem, p_done.now(i, l - 1))
                    dve.wait_ge(r_done.sem, r_done.now(i, 2 * (l - 1) + g))
                right = halves(rb[:, parity, blocks, :], l)[:, :, :, 1, :]
                left_decay = decay_view(parity, l)[:, blocks, 0::2]
                dve.tensor_tensor(right, right, by(left_decay, right.shape),
                                  ALU.mult).then_inc(r_done.sem, 1)

            def copy_level(i, parity, l, g):
                dve.wait_ge(a_done.sem, a_done.now(i, 2 * l + g))
                if l:
                    dve.wait_ge(cp_done.sem, cp_done.now(i, 2 * (l - 1) + g))
                hop(dve, passed)
                dst = halves(at[:, parity, H // 2 * g:H // 2 * (g + 1), :], l)[:, :, :, 1, :]
                n = HALF >> l
                msk = masks[:, l, :].rearrange("p (j q) -> p j q", j=n).unsqueeze(1)
                src = bank_pair(l)[g][:].rearrange("p (h j q) -> p h j q", h=H // 2, j=n)
                dve.copy_predicated(dst, msk.to_broadcast(dst.shape), src).then_inc(cp_done.sem, 1)

            def add_state(i, parity, n):
                dve.wait_ge(s_mult.sem, s_mult.now(i - 1))
                dve.wait_ge(s_done.sem, s_done.now(i - 1, n))
                for j in range(2):
                    rows = slice(HEAD * j, HEAD * j + HEAD)
                    own = state[rows, parity, GB * n:GB * n + GB, rows]
                    got = ps_s[rows, :].rearrange("p (b m) -> p b m", m=P)[:, :, rows]
                    dve.tensor_tensor(own, own, got, ALU.add).then_inc(s_added.sem, 1)

            def outputs(i, n):
                cols = slice(512 * n, 512 * n + 512)
                dve.wait_ge(o_done.sem, o_done.now(i - 1, n))
                dve.wait_ge(dv_done.sem, dv_done.now(i - 1))
                dve.wait_ge(gn.sem, old(gn, i, 2, 2))
                dve.tensor_tensor(ob[:, cols], ps_o[n][:], dv[:, cols], ALU.add).then_inc(o_read.sem, 1)

            def head_means(i):
                dve.wait_ge(o_read.sem, o_read.now(i - 1))
                dve.wait_ge(gn.sem, old(gn, i, 2))
                dve.tensor_reduce(gsum[:], heads(ob[:]), AX_X, ALU.add).then_inc(gn.sem, 1)
                dve.wait_ge(gn.sem, gn.now(i - 1, 0))
                dve.tensor_scalar(gmean[:], gsum[:], 1.0 / HEAD, None, ALU.mult).then_inc(gn.sem, 1)
                dve.wait_ge(gn.sem, gn.now(i - 1, 1))
                dve.wait_ge(n_done.sem, old(n_done, i, 2))
                dve.tensor_tensor(heads(cen[:]), heads(ob[:]), by(gmean[:], head_cols),
                                  ALU.subtract).then_inc(gn.sem, 1)

            def head_variances(i):
                dve.wait_ge(sq_done.sem, sq_done.now(i - 2))
                dve.wait_ge(rooted.sem, old(rooted, i, 3))
                dve.tensor_reduce(gvar[:], heads(sq[:]), AX_X, ALU.add).then_inc(gn.sem, 1)
                dve.wait_ge(gn.sem, gn.now(i - 2, 3))
                dve.tensor_scalar(gve[:], gvar[:], 1.0 / HEAD, GN_EPS, ALU.mult, ALU.add).then_inc(gn.sem, 1)

            def head_scales(i):
                dve.wait_ge(rooted.sem, rooted.now(i - 2))
                dve.wait_ge(n_done.sem, old(n_done, i, 3))
                dve.reciprocal(grs[:], gsd[:]).then_inc(gn.sem, 1)

            def gate(i, pair, parity):
                dve.wait_ge(yt_done.sem, yt_done.now(i - 3))
                dve.wait_ge(g_loaded[1 - parity], 16 * (use_of(pair, parity, -3) + 1))
                dve.wait_ge(y_stored.sem, old(y_stored, i, 4))
                dve.tensor_tensor(yb[:], yt[:], gb[:, 1 - parity], ALU.mult).then_inc(y_done.sem, 1)

            block_decays(0, 0, 0, 0)
            for g in range(2):
                scale_r(0, 0, 0, g)

            def body(i, pair, parity):
                if has(i):
                    dve.wait_ge(o_done.sem, old(o_done, i, 2))
                    dve.wait_ge(wide_done.sem, old(wide_done, i, 2))
                for l in range(LEVELS):
                    if l == LEVELS - 1 and has(i, 1):
                        head_means(i)
                    for g in range(2):
                        if has(i) and l + 1 < LEVELS:
                            scale_r(i, parity, l + 1, g)
                        if l == LEVELS - 1 and has(i) and has(i, -1):
                            scale_r(i + 1, 1 - parity, 0, g)
                    for g in range(2 if has(i) and l < MASKED else 0):
                        copy_level(i, parity, l, g)
                    if l == 0 and has(i, 2):
                        head_variances(i)
                    if l in (1, 3) and has(i, 1):
                        add_state(i, parity, l // 2)
                    if l == 1 and has(i, 2):
                        head_scales(i)
                    if l in (2, 4) and has(i, 1):
                        outputs(i, l // 2 - 1)
                    if l == 2 and has(i, 3):
                        gate(i, pair, parity)
                    if l == 5 and has(i) and has(i, -1):
                        block_decays(i, pair, parity, 1)

            steps(dve, body)

        @block.scalar
        def _(act):
            for s in (d_copied, rbd_done, sq_done, wide_done, rooted, yt_done, kt_copied):
                s.grant(act)
            act.wait_ge(consts, 16 * 6)
            act.wait_ge(zeroed, 5)

            def place_r(i, parity, l, g):
                if l:
                    act.wait_ge(r_done.sem, r_done.now(i, 2 * (l - 1) + g))
                if l >= 2:
                    act.wait_ge(a_done.sem, a_done.now(i, 2 * (l - 2) + g))
                else:
                    act.wait_ge(a_done.sem, a_done.now(i - 1, 2 * (LEVELS - 2 + l) + g))
                for j in range(2):
                    rows = slice(HEAD * j, HEAD * j + HEAD)
                    right = halves(rb[rows, parity, GB * g:GB * g + GB, :], l)[:, :, :, 1, :]
                    dst = rbd[rows, (l + parity) % 2, GB * g:GB * g + GB, HALF * j:HALF * j + HALF]
                    act.copy(dst.rearrange("p b (j q) -> p b j q", q=1 << l), right).then_inc(rbd_done.sem, 1)

            def place_first(i, pair, parity, of):
                q = (parity + of) % 2
                act.wait_ge(rv_loaded[q], 32 * (use_of(pair, parity, of) + 1))
                for g in range(2):
                    place_r(i + of, q, 0, g)

            def copy_wide(i, parity, l, g):
                act.wait_ge(a_done.sem, a_done.now(i, 2 * l + g))
                act.wait_ge(cp_done.sem, cp_done.now(i, 2 * (MASKED - 1) + g))
                size = 1 << l
                for n, (low, high) in enumerate(UNMASKED[l]):
                    src = bank_pair(l)[g][low:high, :].rearrange("p (h t) -> p h t", h=H // 2)
                    dst = at[low:high, parity, H // 2 * g:H // 2 * (g + 1), low + size:high + size]
                    copied = act.copy(dst, src[:, :, n * size:n * size + size])
                copied.then_inc(wide_done.sem, 1)

            def scale_norm(i, g):
                act.wait_ge(y_done.sem, old(y_done, i, 3))
                act.wait_ge(nt_done.sem, nt_done.now(i - 2, g))
                for b in range(GB * g, GB * g + GB):
                    act.activation(yt[:, b, :], ps_o[g][:, (b % GB) * P:(b % GB + 1) * P], ACT.Identity,
                                   bias=bet[:, b:b + 1], scale=gam[:, b:b + 1]).then_inc(yt_done.sem, 1)

            def turn_k(i):
                for g in range(2):
                    act.wait_ge(kt_done.sem, kt_done.now(i - 1, g))
                    act.wait_ge(s_done.sem, old(s_done, i, 2, g))
                    act.copy(kt[:, 512 * g:512 * g + 512], bank_pair(KT)[g][:]).then_inc(kt_copied.sem, 1)

            place_first(0, 0, 0, 0)

            def body(i, pair, parity):
                if has(i, 1):
                    turn_k(i)
                for l in range(1, LEVELS):
                    for g in range(2 if has(i) else 0):
                        place_r(i, parity, l, g)
                    if l == 1 and has(i, 2):
                        act.wait_ge(gn.sem, gn.now(i - 2, 2))
                        act.activation(sq[:], cen[:], ACT.Square).then_inc(sq_done.sem, 1)
                    if l == 2 and has(i, 2):
                        act.wait_ge(gn.sem, gn.now(i - 2, 4))
                        act.activation(gsd[:], gve[:], ACT.Sqrt).then_inc(rooted.sem, 1)
                    if l == 3 and has(i):
                        act.wait_ge(d_done.sem, d_done.now(i))
                        act.wait_ge(dv_done.sem, dv_done.now(i - 1))
                        act.copy(dsb[:], ps_d[:]).then_inc(d_copied.sem, 1)
                if has(i, 2):
                    scale_norm(i, 0)
                if has(i) and has(i, -1):
                    place_first(i, pair, parity, 1)
                if has(i):
                    for l in (5, 6):
                        for g in range(2):
                            copy_wide(i, parity, l, g)
                if has(i, 2):
                    scale_norm(i, 1)

            steps(act, body)

        @block.tensor
        def _(pe):
            for s in (d_done, a_done, nt_done, kt_done, s_done, o_done):
                s.grant(pe)
            pe.wait_ge(consts, 16 * 6)
            pe.wait_ge(zeroed, 5)

            def level(i, pair, parity, l):
                if l == 0:
                    pe.wait_ge(kw_loaded[parity], 32 * (pair + 1))
                for g in range(2):
                    wait_bank(pe, l, i, g)
                    pe.wait_ge(rbd_done.sem, rbd_done.now(i, 4 * l + 2 * g + 1))
                    if l:
                        pe.wait_ge(k_done.sem, k_done.now(i, 2 * (l - 1) + g))
                    for b in range(GB * g, GB * g + GB):
                        mm = pe.matmul(bank_pair(l)[g][:, (b % GB) * P:(b % GB + 1) * P],
                                       kb[:, parity, b, :], rbd[:, (l + parity) % 2, b, :], start=True, stop=True)
                    mm.then_inc(a_done.sem, 1)

            def bonus_sums(i):
                pe.wait_ge(rk_done.sem, rk_done.now(i))
                pe.wait_ge(d_copied.sem, d_copied.now(i - 1))
                for b in range(CB):
                    mm = pe.matmul(ps_d[:, 2 * b:2 * b + 2], rk[:, b, :], bonus[:, b, :], start=True, stop=True)
                mm.then_inc(d_done.sem, 1)

            def state_part(i, parity, n):
                pe.wait_ge(kt_copied.sem, kt_copied.now(i - 1, n))
                pe.wait_ge(s_added.sem, s_added.now(i - 1, 1) if n else old(s_added, i, 2))
                for b in range(GB * n, GB * n + GB):
                    cols = slice(b * P, b * P + P)
                    mm = pe.matmul(ps_s[:, (b % GB) * P:(b % GB + 1) * P], kt[:, cols], vb[:, parity, cols],
                                   start=True, stop=True)
                mm.then_inc(s_done.sem, 1)

            def outputs(i, parity, quarter):
                n, second = divmod(quarter, 2)
                if not second:
                    pe.wait_ge(yt_done.sem, old(yt_done, i, 3, GB * n + GB - 1))
                    pe.wait_ge(o_read.sem, old(o_read, i, 2, n))
                    pe.wait_ge(r_done.sem, r_done.now(i - 1))
                    pe.wait_ge(cp_done.sem, cp_done.now(i - 1, 2 * (MASKED - 1) + n))
                    pe.wait_ge(wide_done.sem, wide_done.now(i - 1, 2 * (LEVELS - 1 - MASKED) + n))
                for b in range(2 * quarter, 2 * quarter + 2):
                    at_col = (b % GB) * P
                    pe.matmul(ps_o[n][:, at_col:at_col + P], rb[:, parity, b, :], state[:, parity, b, :],
                              start=True, stop=False)
                    for j in range(2):
                        head = 2 * b + j
                        mm = pe.matmul(ps_o[n][:, at_col + HEAD * j:at_col + HEAD * j + HEAD],
                                       at[:, parity, head, :], vb[:, parity, head * HEAD:(head + 1) * HEAD],
                                       start=False, stop=j == 1)
                if second:
                    mm.then_inc(o_done.sem, 1)

            def turn_norm(i, g):
                pe.wait_ge(n_done.sem, n_done.now(i - 2))
                if has(i, 1):
                    pe.wait_ge(o_read.sem, o_read.now(i - 1, g))
                else:
                    pe.wait_ge(yt_done.sem, yt_done.now(i - 3))
                for b in range(GB * g, GB * g + GB):
                    mm = pe.transpose(ps_o[g][:, (b % GB) * P:(b % GB + 1) * P], nrm[:, b * P:(b + 1) * P], ident[:])
                mm.then_inc(nt_done.sem, 1)

            def turn_k(i, parity):
                for g in range(2):
                    wait_bank(pe, KT, i, g)
                    pe.wait_ge(k_done.sem, k_done.now(i, 2 * (LEVELS - 1) + g))
                    for b in range(GB * g, GB * g + GB):
                        mm = pe.transpose(bank_pair(KT)[g][:, (b % GB) * P:(b % GB + 1) * P],
                                          kb[:, parity, b, :], ident[:])
                    mm.then_inc(kt_done.sem, 1)

            def body(i, pair, parity):
                for l in range(LEVELS):
                    if has(i):
                        level(i, pair, parity, l)
                    if has(i, 1):
                        if l in (0, 2):
                            state_part(i, 1 - parity, l // 2)
                        if l < 4:
                            outputs(i, 1 - parity, l)
                    if l == 1 and has(i):
                        bonus_sums(i)
                    if l in (4, 5) and has(i, 2):
                        turn_norm(i, l - 4)
                if has(i):
                    turn_k(i, parity)

            steps(pe, body)


def level_masks():
    import numpy as np

    s = np.arange(CHUNK)[:, None]
    masks = []
    for level in range(LEVELS):
        size = 1 << level
        t = np.arange(CHUNK).reshape(-1, 2, size)[:, 1].reshape(1, -1)
        masks.append((s // (2 * size) == t // (2 * size)) & (s // size % 2 == 0))
    return np.ascontiguousarray(np.stack(masks, 1).astype(np.int32))


def output_phase(nc, yT, x, w_o, factors_sum, bias, ident_dram, out):
    with ExitStack() as ctx:
        sb = lambda name, shape, dt=F32: ctx.enter_context(nc.sbuf_tensor("o_" + name, shape, dt))
        ps = lambda name: ctx.enter_context(nc.psum_tensor("o_" + name, [P, 512], F32))
        phase = ctx.enter_context(Phase(nc, "o_"))
        sig, sem = phase.counter, phase.semaphore
        NT = T // P
        GB = CB // 2
        wo_hi, wo_lo, wf_hi, wf_lo = (sb(n, [P, CB, C], F32R) for n in ("wohi", "wolo", "wfhi", "wflo"))
        split_load, split_high, split_low, w_low = load_split(
            nc, ctx, phase, [(w_o, wo_hi, wo_lo), (factors_sum, wf_hi, wf_lo)])
        ident = sb("ident", [P, P])
        brow = sb("brow", [P, C])
        yb = sb("yb", [P, CB, P])
        y_hi, y_lo = sb("yhi", [P, 2, CB, P], F32R), sb("ylo", [P, 2, CB, P], F32R)
        xb = sb("xb", [P, C])
        x1 = sb("x1", [P, C])
        x1b = sb("x1b", [P, 2, C])
        stats, mv = sb("stats", [P, 12]), sb("mv", [P, 2])
        eps, sd, rstd, nmr = (sb(n, [P, 1]) for n in ("eps", "sd", "rstd", "nmr"))
        h2 = sb("h2", [P, C])
        h_hi, h_lo = sb("hhi", [P, CB, P], F32R), sb("hlo", [P, CB, P], F32R)
        fin = sb("fin", [P, C])
        ps_o, ps_f, ps_t = ([ps(f"{n}{g}") for g in range(2)] for n in "oft")

        consts, zeroed, passed = sem("consts"), sem("zeroed"), sem("passed")
        y_loaded, x_loaded = sem("y_loaded"), sem("x_loaded")
        stored = sig("stored", 16)
        o_done, f_done, t_done = sig("o_done", 2), sig("f_done", 2), sig("t_done", 2)
        ylo_done, x1_done, stat, aggr = sig("ylo_done"), sig("x1_done", 2), sig("stat", 2), sig("aggr")
        scaled, hlo_done, fin_done = sig("scaled", 2), sig("hlo_done", 2), sig("fin_done", 2)
        yhi_done, rooted, h2_done, hhi_done = sig("yhi_done"), sig("rooted"), sig("h2_done"), sig("hhi_done", 2)
        x1b_done = sig("x1b_done")
        block = ctx.enter_context(nc.Block())

        def steps(eng, body):
            for i in (0, 1):
                body(i, i)
            with eng.Fori(1, NT // 2 - 1) as pair:
                for parity in range(2):
                    body(2 * pair + parity, parity)
            for i in range(NT - 2, NT + 2):
                body(i, i % 2)

        def factors_pieces(i):
            return range(CB + i * CB // 2, CB + (i + 1) * CB // 2) if isinstance(i, int) and i < 2 else ()

        def has(i, back):
            return not isinstance(i, int) or 0 <= i - back < NT

        def old(signal, i, back, k=None):
            if isinstance(i, int) and i - back < -1:
                return signal.now(-1)
            return signal.now(i - back, k)

        @block.sync
        def _(sp):
            stored.grant(sp)
            sp.dma_start(ident[:], ident_dram).then_inc(consts, 16)
            sp.dma_start(brow[:], bias.rearrange("(a n) -> a n", a=1).to_broadcast([P, C])).then_inc(consts, 16)

            def load_y(i):
                sp.wait_ge(ylo_done.sem, old(ylo_done, i, 1))
                sp.dma_start(yb[:], yT[:, :, bass.ds(i * P, P)]).then_inc(y_loaded, 16)

            load_y(0)
            split_load(sp, range(CB))

            def body(i, parity):
                if has(i, -1):
                    load_y(i + 1)
                if has(i, 0):
                    sp.wait_ge(x1_done.sem, old(x1_done, i, 1))
                    sp.dma_start(xb[:], x[bass.ds(i * P, P), :]).then_inc(x_loaded, 16)
                split_load(sp, factors_pieces(i))
                if has(i, 2):
                    sp.wait_ge(fin_done.sem, fin_done.now(i - 2))
                    sp.dma_start(out[bass.ds((i - 2) * P, P), :], fin[:]).then_inc(stored.sem, 16)

            steps(sp, body)
            sp.wait_ge(stored.sem, stored.now(NT - 1))

        @block.gpsimd
        def _(pool):
            x1b_done.grant(pool)
            pool.wait_ge(consts, 32)

            def body(i, parity):
                if has(i, 0):
                    pool.wait_ge(x1_done.sem, x1_done.now(i))
                    pool.wait_ge(fin_done.sem, old(fin_done, i, 2))
                    pool.tensor_tensor(x1b[:, parity], x1[:], brow[:], ALU.add).then_inc(x1b_done.sem, 1)

            steps(pool, body)

        @block.vector
        def _(dve):
            for s in (ylo_done, x1_done, stat, aggr, scaled, hlo_done, fin_done):
                s.grant(dve)
            dve.memset(eps[:], LN_EPS).then_inc(zeroed, 1)

            def y_low(i, parity):
                dve.wait_ge(yhi_done.sem, yhi_done.now(i))
                dve.tensor_tensor(y_lo[:, parity], yb[:], y_hi[:, parity].bitcast(F32),
                                  ALU.subtract).then_inc(ylo_done.sem, 1)

            y_low(0, 0)
            split_low(dve, range(CB))

            def body(i, parity):
                if has(i, 1):
                    for g in range(2):
                        dve.wait_ge(hhi_done.sem, hhi_done.now(i - 1, g))
                        blocks = slice(GB * g, GB * g + GB)
                        dve.tensor_tensor(h_lo[:, blocks], ps_t[g][:].rearrange("p (b t) -> p b t", b=GB),
                                          h_hi[:, blocks].bitcast(F32), ALU.subtract).then_inc(hlo_done.sem, 1)

            def main(i, parity):
                if has(i, -1):
                    y_low(i + 1, 1 - parity)
                if has(i, 0):
                    dve.wait_ge(h2_done.sem, old(h2_done, i, 1))
                    dve.wait_ge(x1b_done.sem, old(x1b_done, i, 1))
                    dve.wait_ge(x_loaded, 16 * (i + 1))
                    for g in range(2):
                        cols = slice(512 * g, 512 * g + 512)
                        dve.wait_ge(o_done.sem, o_done.now(i, g))
                        dve.tensor_tensor(x1[:, cols], ps_o[g][:], xb[:, cols], ALU.add).then_inc(x1_done.sem, 1)
                    dve.wait_ge(aggr.sem, old(aggr, i, 1))
                    for g in range(2):
                        dve.wait_ge(x1_done.sem, x1_done.now(i, g))
                        dve.bn_stats(stats[:, 6 * g:6 * g + 6], x1[:, 512 * g:512 * g + 512]).then_inc(stat.sem, 1)
                    dve.wait_ge(stat.sem, stat.now(i))
                    dve.wait_ge(scaled.sem, old(scaled, i, 1))
                    hop(dve, passed)
                    dve.bn_aggr(mv[:], stats[:]).then_inc(aggr.sem, 1)
                    dve.wait_ge(rooted.sem, rooted.now(i))
                    dve.reciprocal(rstd[:], sd[:]).then_inc(scaled.sem, 1)
                    dve.wait_ge(scaled.sem, scaled.now(i, 0))
                    dve.scalar_tensor_tensor(nmr[:], mv[:, 0:1], -1.0, rstd[:], ALU.mult,
                                             ALU.mult).then_inc(scaled.sem, 1)
                if has(i, 2):
                    dve.wait_ge(x1b_done.sem, x1b_done.now(i - 2))
                    dve.wait_ge(stored.sem, stored.now(i - 3))
                    for g in range(2):
                        cols = slice(512 * g, 512 * g + 512)
                        dve.wait_ge(f_done.sem, f_done.now(i - 2, g))
                        dve.scalar_tensor_tensor(fin[:, cols], ps_f[g][:], float(RANK) ** -0.5, x1b[:, parity, cols],
                                                 ALU.mult, ALU.add).then_inc(fin_done.sem, 1)
                body(i, parity)
                split_low(dve, factors_pieces(i))

            steps(dve, main)

        @block.scalar
        def _(act):
            for s in (yhi_done, rooted, h2_done, hhi_done):
                s.grant(act)
            act.wait_ge(zeroed, 1)

            def y_high(i, parity):
                act.wait_ge(y_loaded, 16 * (i + 1))
                act.wait_ge(o_done.sem, old(o_done, i, 2))
                act.copy(y_hi[:, parity], yb[:]).then_inc(yhi_done.sem, 1)

            y_high(0, 0)
            split_high(act, range(CB))

            def body(i, parity):
                if has(i, -1):
                    y_high(i + 1, 1 - parity)
                if has(i, 0):
                    act.wait_ge(aggr.sem, aggr.now(i))
                    act.activation(sd[:], mv[:, 1:2], ACT.Sqrt, bias=eps[:]).then_inc(rooted.sem, 1)
                    act.wait_ge(scaled.sem, scaled.now(i))
                if has(i, 1):
                    for g in range(2):
                        act.wait_ge(t_done.sem, t_done.now(i - 1, g))
                        act.wait_ge(f_done.sem, old(f_done, i, 2))
                        act.copy(h_hi[:, GB * g:GB * g + GB], ps_t[g][:].rearrange("p (b t) -> p b t", b=GB)
                                 ).then_inc(hhi_done.sem, 1)
                if has(i, 0):
                    act.wait_ge(t_done.sem, old(t_done, i, 1))
                    act.activation(h2[:], x1[:], ACT.Identity, bias=nmr[:], scale=rstd[:]).then_inc(h2_done.sem, 1)
                split_high(act, factors_pieces(i))

            steps(act, body)

        @block.tensor
        def _(pe):
            for s in (o_done, f_done, t_done):
                s.grant(pe)
            pe.wait_ge(consts, 32)

            def product(banks, left_hi, left_lo, right_hi, right_lo, done):
                for g in range(2):
                    cols = slice(512 * g, 512 * g + 512)
                    for b in range(CB):
                        pe.matmul(banks[g][:], left_hi[:, b, :], right_hi[:, b, cols], start=b == 0, stop=False)
                        pe.matmul(banks[g][:], left_hi[:, b, :], right_lo[:, b, cols], start=False, stop=False)
                        mm = pe.matmul(banks[g][:], left_lo[:, b, :], right_hi[:, b, cols], start=False,
                                       stop=b == CB - 1)
                    mm.then_inc(done.sem, 1)

            pe.wait_ge(w_low, CB)

            def body(i, parity):
                if has(i, 0):
                    pe.wait_ge(ylo_done.sem, ylo_done.now(i))
                    pe.wait_ge(x1_done.sem, old(x1_done, i, 1))
                    product(ps_o, y_hi[:, parity], y_lo[:, parity], wo_hi, wo_lo, o_done)
                if has(i, 2):
                    pe.wait_ge(hlo_done.sem, hlo_done.now(i - 2))
                    pe.wait_ge(fin_done.sem, old(fin_done, i, 3))
                    product(ps_f, h_hi, h_lo, wf_hi, wf_lo, f_done)
                if has(i, 1):
                    pe.wait_ge(h2_done.sem, h2_done.now(i - 1))
                    for g in range(2):
                        pe.wait_ge(hlo_done.sem, old(hlo_done, i, 2, g))
                        for b in range(GB * g, GB * g + GB):
                            mm = pe.transpose(ps_t[g][:, (b % GB) * P:(b % GB + 1) * P], h2[:, b * P:(b + 1) * P],
                                              ident[:])
                        mm.then_inc(t_done.sem, 1)
                if isinstance(i, int) and i == 1:
                    pe.wait_ge(w_low, 2 * CB)

            steps(pe, body)


def build(nc, a, out):
    def scratch(name, shape):
        return nc.dram_tensor(name, shape, F32, kind="Internal").ap()

    blocks = lambda ap: ap.rearrange("(b p) n -> p b n", p=P)
    hT, zs = blocks(scratch("hT", [C, T + 1])), scratch("zs", [NMIX, 3 * DMIX, T])
    factors_sum = scratch("factors_sum", [C, C])
    rT, kT, gT, wT, yT = (blocks(scratch(n, [C, T])) for n in ("rT", "kT", "gT", "wT", "yT"))
    v = scratch("v", [T, C])
    norm_phase(nc, a["hidden"], a["time_maa_x"], a["time_maa_w1"], a["ident"], hT, zs)
    decay_phase(nc, hT, zs[0], a["time_maa_w2"][0], a["time_maa_w"], a["time_decay_w1"], a["time_decay_w2"],
                a["time_decay"], wT)
    streams = [(kind, n, a["time_maa_" + what], blocks(a["W_" + what]), dst) for kind, n, what, dst in (
        ("rk", 1, "k", kT), ("rk", 3, "r", rT), ("g", 4, "g", gT), ("v", 2, "v", v))]
    streams_phase(nc, hT, zs, a["time_maa_w2"], streams, a["factors"], factors_sum)
    recurrence_phase(nc, rT, kT, wT, gT, v, a["time_faaaa"], a["ln_gamma"], a["ln_beta"], a["ident"], a["masks"], yT)
    output_phase(nc, yT, a["hidden"], blocks(a["W_o"]), blocks(factors_sum), a["bias"], a["ident"], out)


def kernel(**inputs):
    import numpy as np
    import concourse.bacc as bacc
    from concourse.bass_utils import run_bass_kernel_spmd

    given = {}
    for name, value in inputs.items():
        short = name.removeprefix("L0_attn_").removeprefix("L0_ffn_")
        value = np.asarray(value)
        if short.startswith("W_"):
            value = value.T
        elif short == "hidden":
            value = value[0]
        elif short.startswith("time_maa_") and value.ndim == 3 and value.shape[0] == 1 or short == "time_decay":
            value = value.reshape(-1)
        given[short] = np.ascontiguousarray(value)
    given["ident"] = np.eye(P, dtype=np.float32)
    given["masks"] = level_masks()

    nc = bacc.Bacc("TRN2", target_bir_lowering=False, num_devices=1)
    arrays, aps = {}, {}
    for name, value in given.items():
        arrays[f"in_{name}"] = value
        aps[name] = nc.dram_tensor(f"in_{name}", value.shape, mybir.dt.from_np(value.dtype), kind="ExternalInput").ap()
    out = nc.dram_tensor("out", [T, C], F32, kind="ExternalOutput").ap()
    build(nc, aps, out)
    results = run_bass_kernel_spmd(nc, [arrays], core_ids=[0])
    return results.results[0]["out"].reshape(1, T, C)
```
